# Optimizing a Trainium2 kernel written in Bass

```python
import numpy as np
import jax
import jax.numpy as jnp

def _softmax(x, axis=-1):
    return jax.nn.softmax(x, axis=axis)

def _gelu(x):
    return jax.nn.gelu(x, approximate=True)

def _silu(x):
    return jax.nn.silu(x)

def _sigmoid(x):
    return jax.nn.sigmoid(x)

def _layernorm(x, axis=-1, eps=1e-05):
    m = jnp.mean(x, axis=axis, keepdims=True)
    v = jnp.var(x, axis=axis, keepdims=True)
    return (x - m) / jnp.sqrt(v + eps)

def _scatter_add(tgt, idx, src, axis=0):
    return tgt.at[idx].add(src)

def _segment_sum(src, seg, n):
    return jax.ops.segment_sum(src, seg, n)
kernel_name = 'mk_xattn_ffn_d1_seqx_r8_c8794e'

def setup_inputs(seed: int=0):
    np.random.seed(seed)
    _w = jnp.asarray

    def _rec_inputs():
        import jax
        import jax.numpy as jnp
        _rk = jax.random.key(seed)
        x = 0.0001212 + 1 * jax.random.normal(jax.random.fold_in(_rk, 1), (64, 64, 256), jnp.float32)
        _lenS = 64 - jax.random.randint(jax.random.fold_in(_rk, 7), (64,), 0, max(1, 64 // 4) + 1, jnp.int32)
        _lenS2 = 64 - jax.random.randint(jax.random.fold_in(_rk, 8), (64,), 0, max(1, 64 // 4) + 1, jnp.int32)
        _ctx_2048P = jax.random.normal(jax.random.fold_in(_rk, 11), (64, 16, 256), jnp.float32)
        _ctx_2048c = jax.random.dirichlet(jax.random.fold_in(_rk, 511), 0.3 * jnp.ones((16,), jnp.float32), (64, 64))
        _ctx_2048t = jnp.einsum('bsk,bkd->bsd', _ctx_2048c, _ctx_2048P)
        _ctx_2048t = _ctx_2048t * jax.lax.rsqrt(jnp.mean(jnp.square(_ctx_2048t)) + 1e-12) * 0.953939
        ctx_2048 = 0.000173663 + 1.0001 * (_ctx_2048t + 0.3 * jax.random.normal(jax.random.fold_in(_rk, 611), (64, 64, 256), jnp.float32))
        return (x, ctx_2048)
    x, ctx_2048 = _rec_inputs()

    def _L0_xattn_setup():
        import jax, jax.numpy as jnp
        import numpy as np
        B_DIM, T_DIM, C_DIM = (16, 128, 256)

        def _wkv(w, u, k, v):
            Bn, Tn, Cn = k.shape
            NEG_INF = jnp.float32(-1e+38)

            def step(carry, kv_t):
                p, q, o = carry
                kt, vt = kv_t
                no = jnp.maximum(o, u + kt)
                A = jnp.exp(o - no)
                E = jnp.exp(u + kt - no)
                y = (A * p + E * vt) / (A * q + E)
                no2 = jnp.maximum(w + o, kt)
                A2 = jnp.exp(w + o - no2)
                E2 = jnp.exp(kt - no2)
                return ((A2 * p + E2 * vt, A2 * q + E2, no2), y)
            init = (jnp.zeros((Bn, Cn), k.dtype), jnp.zeros((Bn, Cn), k.dtype), jnp.full((Bn, Cn), NEG_INF, k.dtype))
            kT = jnp.moveaxis(k, 1, 0)
            vT = jnp.moveaxis(v, 1, 0)
            _, yT = jax.lax.scan(step, init, (kT, vT))
            return jnp.moveaxis(yT, 0, 1)
        key = jax.random.key(seed)
        k1, k2, k3, k4 = jax.random.split(key, 4)
        w = -jnp.exp(jax.random.normal(k1, (C_DIM,), jnp.float32))
        u = jax.random.normal(k2, (C_DIM,), jnp.float32)
        k = jax.random.normal(k3, (B_DIM, T_DIM, C_DIM), jnp.float32)
        v = jax.random.normal(k4, (B_DIM, T_DIM, C_DIM), jnp.float32)
        return {'B': B_DIM, 'T': T_DIM, 'C': C_DIM, 'w': w, 'u': u, 'k': k, 'v': v}
    _L0_xattn_all = _L0_xattn_setup()
    _L0_xattn_in = {k: v for k, v in _L0_xattn_all.items() if k in ('w', 'u')}
    del _L0_xattn_all

    def _L0_ffn_setup():
        import jax, jax.numpy as jnp
        import numpy as np
        B, S, H, I, E = (2, 256, 256, 176, 8)
        TOP_K = 2
        key = jax.random.key(seed)
        k0, k1, k2, k3, k4 = jax.random.split(key, 5)
        scale = float(np.sqrt(2.0 / (H + I)))
        return {'hidden_states': jax.random.normal(k0, (B, S, H), dtype=jnp.float32), 'router_w': jax.random.normal(k1, (E, H), dtype=jnp.float32) * H ** (-0.5), 'gate_w': jax.random.normal(k2, (E, I, H), dtype=jnp.float32) * scale, 'up_w': jax.random.normal(k3, (E, I, H), dtype=jnp.float32) * scale, 'down_w': jax.random.normal(k4, (E, H, I), dtype=jnp.float32) * scale}
    _L0_ffn_all = _L0_ffn_setup()
    _L0_ffn_in = {k: v for k, v in _L0_ffn_all.items() if k in ('router_w', 'gate_w', 'up_w', 'down_w')}
    del _L0_ffn_all
    return {'x': x, 'ctx_2048': ctx_2048, 'L0_xattn_w': _L0_xattn_in['w'], 'L0_xattn_u': _L0_xattn_in['u'], 'L0_ffn_router_w': _L0_ffn_in['router_w'], 'L0_ffn_gate_w': _L0_ffn_in['gate_w'], 'L0_ffn_up_w': _L0_ffn_in['up_w'], 'L0_ffn_down_w': _L0_ffn_in['down_w']}

def reference(x, ctx_2048, L0_xattn_w, L0_xattn_u, L0_ffn_router_w, L0_ffn_gate_w, L0_ffn_up_w, L0_ffn_down_w):
    import jax
    import jax.numpy as jnp

    def _L0_xattn_ref(B, T, C, w, u, k, v):
        import jax, jax.numpy as jnp
        import numpy as np
        B_DIM, T_DIM, C_DIM = (16, 128, 256)

        def _wkv(w, u, k, v):
            Bn, Tn, Cn = k.shape
            NEG_INF = jnp.float32(-1e+38)

            def step(carry, kv_t):
                p, q, o = carry
                kt, vt = kv_t
                no = jnp.maximum(o, u + kt)
                A = jnp.exp(o - no)
                E = jnp.exp(u + kt - no)
                y = (A * p + E * vt) / (A * q + E)
                no2 = jnp.maximum(w + o, kt)
                A2 = jnp.exp(w + o - no2)
                E2 = jnp.exp(kt - no2)
                return ((A2 * p + E2 * vt, A2 * q + E2, no2), y)
            init = (jnp.zeros((Bn, Cn), k.dtype), jnp.zeros((Bn, Cn), k.dtype), jnp.full((Bn, Cn), NEG_INF, k.dtype))
            kT = jnp.moveaxis(k, 1, 0)
            vT = jnp.moveaxis(v, 1, 0)
            _, yT = jax.lax.scan(step, init, (kT, vT))
            return jnp.moveaxis(yT, 0, 1)
        return _wkv(w, u, k, v)

    def _L0_ffn_ref(hidden_states, router_w, gate_w, up_w, down_w):
        import jax, jax.numpy as jnp
        import numpy as np
        B, S, H, I, E = (2, 256, 256, 176, 8)
        TOP_K = 2
        b, s, h = hidden_states.shape
        e = router_w.shape[0]
        x = hidden_states.reshape(-1, h)
        logits = jnp.einsum('th,eh->te', x, router_w)
        top_vals, top_idx = jax.lax.top_k(logits, TOP_K)
        top_w = jax.nn.softmax(top_vals, axis=-1)
        expert = top_idx[:, 0]
        weight = top_w[:, 0]
        gate = jnp.einsum('th,eih->eti', x, gate_w)
        up = jnp.einsum('th,eih->eti', x, up_w)
        act = jax.nn.silu(gate) * up
        out_e = jnp.einsum('eti,ehi->eth', act, down_w)
        combine = jax.nn.one_hot(expert, e, dtype=x.dtype) * weight[:, None]
        out = jnp.einsum('eth,te->th', out_e, combine)
        return out.reshape(b, s, h)
    x = x + _L0_xattn_ref(64, 64, 256, L0_xattn_w, L0_xattn_u, _layernorm(x, axis=-1), ctx_2048)
    x = x + _L0_ffn_ref(_layernorm(x, axis=-1), L0_ffn_router_w, L0_ffn_gate_w, L0_ffn_up_w, L0_ffn_down_w)
    return x

_drawn_inputs = setup_inputs


def setup_inputs(seed=0):
    import zlib

    import numpy as np

    out = dict(_drawn_inputs(seed))
    spreads = {}
    factors = {}
    for name, (base, spread) in spreads.items():
        noise = np.random.default_rng([zlib.crc32(name.encode()), seed]).standard_normal(out[name].shape)
        drawn = base * np.exp(spread * noise) if base else spread * noise
        out[name] = jnp.asarray(drawn.astype(out[name].dtype))
    for name, factor in factors.items():
        out[name] = (out[name] * factor).astype(out[name].dtype)
    return out
```

```python
from contextlib import ExitStack

import numpy as np
import concourse.bass as bass
from concourse import mybir

P = 128
B, T, C = 64, 64, 256
TOK = B * T
G = C // P
NB = 512
BLOCKS = TOK // NB
JT = NB // P
SEQ = NB // T
NT = TOK // P
E, I = 8, 176
IH = I // 2
TILES = (TOK + E * (P - 1)) // P
ROW = C + 4
MEAN, RSTD, GAP = C, C + 1, C + 2
PAD_ID = 2 * TOK
EPS = 1e-5

F32, BF16, I32, U32 = mybir.dt.float32, mybir.dt.bfloat16, mybir.dt.int32, mybir.dt.uint32
ALU = mybir.AluOpType
ACT = mybir.ActivationFunctionType
AX = mybir.AxisListType

K_ID, K_LT, K_IOTA, K_E8, K_TILE, K_P, K_EPS, K_ONE = 0, 128, 256, 384, 392, 424, 425, 426
K_ALL = 427


def constants():
    k = np.zeros((P, K_ALL), np.float32)
    p = np.arange(P)
    k[:, K_ID:K_ID + P] = np.eye(P)
    k[:, K_LT:K_LT + P] = p[:, None] < p[None, :]
    k[:, K_IOTA:K_IOTA + P] = p[None, :]
    k[:, K_E8:K_E8 + E] = np.arange(E) - E
    k[:, K_TILE:K_TILE + NT] = np.arange(NT) - PAD_ID // P
    k[:, K_P] = p
    k[:, K_EPS] = EPS
    k[:, K_ONE] = 1.0
    return k


def build(nc, x, x_t, ctx_t, w, u, router, gate_up_t, down_t, consts, out):
    ctx = ExitStack()
    with ctx:
        def sb(name, shape, dt=F32):
            return ctx.enter_context(nc.sbuf_tensor(name, shape, dt))

        def sem(name):
            return ctx.enter_context(nc.semaphore(name))

        def sems(name, n):
            return [sem(f"{name}{k}") for k in range(n)]

        def wait(eng, s, value):
            if not (isinstance(value, int) and value <= 0):
                eng.wait_ge(s, value)

        scratch = nc.dram_tensor("x2_rows", (TOK, ROW), F32, kind="Internal").ap()

        kc = sb("kc", [P, K_ALL])
        ident = kc[:, K_ID:K_ID + P]
        wgu = sb("wgu", [P, G, E, 2 * I])
        wdn = sb("wdn", [IH, 2, E, C])
        wu = sb("wu", [P, 2, G])
        bonus = sb("bonus", [P, 2, G])
        decay1 = sb("decay1", [P, G])
        ab = sb("ab", [P, 2, G])
        diag = sb("diag", [P, 2, G, P])
        decay = sb("decay", [P, G, NB])
        rw = sb("rw", [E, C])
        rsum = sb("rsum", [E, 1])
        rmean = sb("rmean", [E, 1])
        rwc = sb("rwc", [E, C])
        rwt = sb("rwt", [P, G, E])

        def two(name, shape, dt=F32):
            return [sb(f"{name}{h}", shape, dt) for h in range(2)]

        pool_w = JT * C
        assert TILES * ROW <= 10 * pool_w and G * NB == pool_w
        shared = sb("shared", [P, 10 * pool_w])
        xg = shared[:, 0:TILES * ROW].rearrange("p (n c) -> p n c", c=ROW)

        def pair(n, inner):
            return [shared[:, k * pool_w:(k + 1) * pool_w].rearrange("p (a b) -> p a b", b=inner)
                    for k in (2 * n, 2 * n + 1)]

        xr = pair(0, C)
        xn = pair(1, C)
        xt = pair(2, NB)
        vt = pair(3, NB)
        ek = pair(4, NB)
        ev = two("ev", [P, G, NB])
        sk = two("sk", [P, G, NB])
        sv = two("sv", [P, G, NB])
        rd = two("rd", [P, G, NB])
        yt = two("yt", [P, G, NB])
        x2t = two("x2t", [P, G, NB])
        row = two("row", [P, JT, ROW])
        six1 = two("six1", [P, JT, 6])
        mv1 = two("mv1", [P, JT, 2])
        lnv1 = two("lnv1", [P, JT])
        rstd1 = two("rstd1", [P, JT])
        nmr1 = two("nmr1", [P, JT])
        six2 = two("six2", [P, JT, 6])
        lnv2 = two("lnv2", [P, JT])
        top = two("top", [P, JT, 8])
        gap = two("gap", [P, JT])
        logit = sb("logit", [P, NT, E])

        best = sb("best", [P, NT])
        is_best = sb("is_best", [P, NT, E])
        cand = sb("cand", [P, NT, E])
        first = sb("first", [P, NT])
        hot = sb("hot", [P, E, NT], BF16)
        lt_b = sb("lt_b", [P, P], BF16)
        one_b = sb("one_b", [P, P], BF16)
        iota_b = sb("iota_b", [P, P], BF16)
        same_e = sb("same_e", [P, E, NT])
        ones8 = sb("ones8", [P, E])
        upto = sb("upto", [P, E, NT])
        before = sb("before", [P, E, NT])
        slot3 = sb("slot3", [P, E, NT])
        cnt_i = sb("cnt_i", [P, E], I32)
        nt_i = sb("nt_i", [P, E], I32)
        nt_f = sb("nt_f", [P, E])
        end_f = sb("end_f", [P, E])
        base = sb("base", [P, E])
        slot = sb("slot", [P, NT])
        slot_i = sb("slot_i", [P, NT], I32)
        lo_i = sb("lo_i", [P, NT], I32)
        hi_i = sb("hi_i", [P, NT], I32)
        lo_f = sb("lo_f", [P, NT])
        hi_f = sb("hi_f", [P, NT])
        at_lo = sb("at_lo", [P, NT, P], BF16)
        at_hi = sb("at_hi", [P, NT, TILES])
        num_hi = sb("num_hi", [P, NT, 2, TILES], BF16)
        id_hi = sb("id_hi", [P, TILES])
        id_f = sb("id_f", [P, TILES])
        put_id = sb("put_id", [P, TILES], I32)
        get_id = sb("get_id", [P, TILES], I32)
        past = sb("past", [1, TILES, E])
        expert_f = sb("expert_f", [1, TILES])
        expert = sb("expert", [1, TILES], I32)

        def four(name, shape, dt=F32):
            return [sb(f"{name}{k}", shape, dt) for k in range(4)]

        ng = four("ng", [P, C])
        ngt = four("ngt", [P, G, P])
        sg = four("sg", [P, I])
        hh = four("hh", [P, I])
        hht = four("hht", [IH, 2, P])
        th = four("th", [P, 1])
        wt = four("wt", [P, 1])
        ob = four("ob", [P, C])

        bank = [ctx.enter_context(nc.psum_tensor(f"bank{n}", [P, 512], F32)) for n in range(8)]
        kt_ps, den_ps, num_ps = bank[0:2], bank[2:4], bank[4:6]
        rows_ps = bank[6][:, :].rearrange("p (j c) -> p j c", j=2)
        logit_ps = bank[7][:, 0:JT * E].rearrange("p (j e) -> p j e", e=E)
        rwt_ps = bank[7][:, 0:G * E].rearrange("p (g e) -> p g e", e=E)
        rank_ps = bank[0][:, 0:E * NT].rearrange("p (e i) -> p e i", e=E)
        tot_ps = bank[1][:, 0:E * NT].rearrange("p (e i) -> p e i", e=E)
        id_ps = bank[2][:, 0:2 * TILES]
        ngt_ps, gu_ps, hht_ps, o_ps = bank[0:2], bank[2:4], bank[4:6], bank[6:8]

        const_in, wu_in, rw_in, wgu_in, wdn_in = (sem(n) for n in (
            "const_in", "wu_in", "rw_in", "wgu_in", "wdn_in"))
        setup_v, ab_ready, diag_ready, rwt_tr, rwt_ready = (sem(n) for n in (
            "setup_v", "ab_ready", "diag_ready", "rwt_tr", "rwt_ready"))
        x_in, xt_in, v_in, rows_out = (sems(n, 2) for n in ("x_in", "xt_in", "v_in", "rows_out"))
        six1_ready, mv1_ready, lnv1_ready, rstd1_ready, nmr1_ready, xn_ready = (sems(n, 2) for n in (
            "six1_ready", "mv1_ready", "lnv1_ready", "rstd1_ready", "nmr1_ready", "xn_ready"))
        kt_ready, ek_ready, ev_ready, scan_ready = (sems(n, 2) for n in (
            "kt_ready", "ek_ready", "ev_ready", "scan_ready"))
        den_ready, num_ready, lnd_ready, rd_ready, y0_ready, y_ready, x2t_ready = (sems(n, 2) for n in (
            "den_ready", "num_ready", "lnd_ready", "rd_ready", "y0_ready", "y_ready", "x2t_ready"))
        rows_ready, rows_read, logit_ready, logit_read = (sems(n, 2) for n in (
            "rows_ready", "rows_read", "logit_ready", "logit_read"))
        six2_ready, mv2_ready, lnv2_ready, rstd2_ready, gap_ready, row_ready = (sems(n, 2) for n in (
            "six2_ready", "mv2_ready", "lnv2_ready", "rstd2_ready", "gap_ready", "row_ready"))
        route_v, hot_ready, rank_ready, at_lo_ready, num_hi_ready, id_ready, table_ready = (sem(n) for n in (
            "route_v", "hot_ready", "rank_ready", "at_lo_ready", "num_hi_ready", "id_ready", "table_ready"))
        xg_in, ng_ready, ngt_tr, ngt_ready, gu_ready, sg_ready, hh_ready = (sems(n, 4) for n in (
            "xg_in", "ng_ready", "ngt_tr", "ngt_ready", "gu_ready", "sg_ready", "hh_ready"))
        hht_tr, hht_ready, th_ready, wt_ready, o_ready, ob_ready, put_out = (sems(n, 4) for n in (
            "hht_tr", "hht_ready", "th_ready", "wt_ready", "o_ready", "ob_ready", "put_out"))

        def wait_apart(eng, s, value):
            eng.wait_ge(const_in, 16)
            wait(eng, s, value)

        def back(t, n, slots):
            i, k = t
            k -= n
            while k < 0:
                k += slots
                i = i - 1
            return i, k

        def rows_of(t):
            i, k = t
            return xg[:, bass.ds(4 * i + k, 1), :].rearrange("p o c -> p (o c)")

        def ahead2(t):
            i, h = t
            return (i, 1) if h == 0 else (i + 1, 0)

        def ahead(t, n):
            i, k = t
            return (i, k + n) if k + n < 4 else (i + 1, k + n - 4)

        def run(eng, step, first, loop, last, slots):
            if loop is None:
                for s in range(first, last):
                    step((s // slots, s % slots), s)
                return
            for s in range(first, loop[0] * slots):
                step((s // slots, s % slots), s)
            with eng.Fori(loop[0], loop[1]) as i:
                for k in range(slots):
                    step((i, k), None)
            for s in range(loop[1] * slots, last):
                step((s // slots, s % slots), s)

        LAG = 4
        STEPS = BLOCKS + LAG
        LOOP1 = None
        LOOP3 = (1, TILES // 4)

        def active(s, lag):
            return s is None or 0 <= s - lag < BLOCKS

        def live(s, ahead):
            return s is None or 0 <= s + ahead < TILES

        x_v = x.rearrange("(b j p) c -> p b j c", j=JT, p=P)
        xt_v = x_t.rearrange("(g p) (b n) -> p b g n", p=P, n=NB)
        ct_v = ctx_t.rearrange("(g p) (b n) -> p b g n", p=P, n=NB)
        sc_v = scratch.rearrange("(b j p) c -> p b j c", j=JT, p=P)

        def by_seq(a):
            return a.rearrange("p (s t) -> p s t", t=T)

        blk = ctx.enter_context(nc.Block())

        @blk.sync
        def _(sp):
            sp.dma_start(kc[:, :], consts).then_inc(const_in, 16)
            sp.dma_start(wu[:, 0, :], w).then_inc(wu_in, 16)
            sp.dma_start(wu[:, 1, :], u).then_inc(wu_in, 16)
            sp.dma_start(rw[:, :], router).then_inc(rw_in, 16)

            def load_rows(t):
                i, h = t
                wait(sp, xn_ready[h], i)
                sp.dma_start(xr[h][:, :, :], x_v[:, 2 * i + h]).then_inc(x_in[h], 16)

            def load_ctx(t):
                i, h = t
                wait(sp, ev_ready[h], 2 * i)
                wait(sp, y0_ready[h], i)
                sp.dma_start(vt[h][:, :, :], ct_v[:, 2 * i + h]).then_inc(v_in[h], 16)

            def load_columns(t):
                i, h = t
                wait(sp, x2t_ready[h], 2 * i)
                sp.dma_start(xt[h][:, :, :], xt_v[:, 2 * i + h]).then_inc(xt_in[h], 16)

            def store(t):
                i, h = t
                wait(sp, row_ready[h], i + 1)
                sp.dma_start(sc_v[:, 2 * i + h], row[h][:, :, :]).then_inc(rows_out[h], 16)

            def step(t, s):
                if active(s, -1):
                    load_rows(ahead2(t))
                if active(s, 0):
                    load_ctx(t)
                if s == LAG:
                    sp.dma_start(wgu[:, :, :, :], gate_up_t.rearrange("(g p) e n -> p g e n", p=P)).then_inc(wgu_in, 16)
                    sp.dma_start(wdn[:, :, :, :], down_t.rearrange("(a p) e n -> p a e n", p=IH)).then_inc(wdn_in, 16)
                if active(s, LAG):
                    store(back(t, LAG, 2))
                if active(s, 0):
                    load_columns(t)

            load_rows((0, 0))
            run(sp, step, 0, LOOP1, STEPS, 2)
            for k in range(4):
                wait(sp, put_out[k], 16 * len(range(k, TILES, 4)))

        @blk.gpsimd
        def _(pool):
            def weigh(t):
                i, h = t
                wait(pool, v_in[h], 16 * (i + 1))
                wait(pool, num_ready[h], 2 * i)
                for g in range(G):
                    wait(pool, ek_ready[h], 2 * i + g + 1)
                    nc.gpsimd.tensor_tensor(ev[h][:, g, :], ek[h][:, g, :], vt[h][:, g, :],
                                            ALU.mult).then_inc(ev_ready[h], 1)

            def residual(t):
                i, h = t
                wait(pool, xt_in[h], 16 * (i + 1))
                wait(pool, y0_ready[h], i + 1)
                wait(pool, rows_ready[h], 2 * i)
                wait(pool, logit_ready[h], i)
                for g in range(G):
                    wait(pool, y_ready[h], 2 * i + g + 1)
                    nc.gpsimd.tensor_tensor(x2t[h][:, g, :], yt[h][:, g, :], xt[h][:, g, :],
                                            ALU.add).then_inc(x2t_ready[h], 1)

            def step(t, s):
                if active(s, 1):
                    weigh(back(t, 1, 2))
                if active(s, 2):
                    residual(back(t, 2, 2))

            run(pool, step, 0, LOOP1, STEPS, 2)

            for h in range(2):
                wait(pool, rows_out[h], 16 * (BLOCKS // 2))
            pool.wait_ge(table_ready, 1)

            def gather(n):
                wait(pool, ng_ready[n % 4], n // 4)
                pool.indirect_dma_start(
                    out=xg[:, n, :], out_offset=None, in_=scratch,
                    in_offset=bass.IndirectOffsetOnAxis(ap=get_id[:, n:n + 1], axis=0)).then_inc(xg_in[n % 4], 16)

            def scatter(n):
                wait(pool, ob_ready[n % 4], n // 4 + 1)
                pool.indirect_dma_start(
                    out=out, out_offset=bass.IndirectOffsetOnAxis(ap=put_id[:, n:n + 1], axis=0),
                    in_=ob[n % 4][:, :], in_offset=None, bounds_check=TOK - 1, oob_is_err=False)\
                    .then_inc(put_out[n % 4], 16)

            for n in range(4):
                gather(n)
            for n in range(TILES):
                if n + 4 < TILES:
                    gather(n + 4)
                scatter(n)

        @blk.scalar
        def _(act):
            nc.scalar.preload_act_table_set("natural_log_exp_and_others")
            act.wait_ge(setup_v, 1)
            nc.scalar.activation(decay1[:, :], wu[:, 0, :], ACT.Exp)
            nc.scalar.activation(ab[:, 0, :], bonus[:, 0, :], ACT.Exp, scale=-1.0)
            nc.scalar.activation(ab[:, 1, :], bonus[:, 1, :], ACT.Exp).then_inc(ab_ready, 1)

            def evacuate(t):
                i, h = t
                wait(act, rows_out[h], 16 * i)
                for q in range(2):
                    wait(act, rows_ready[h], 2 * i + q + 1)
                    nc.scalar.activation(row[h][:, 2 * q:2 * q + 2, 0:C], rows_ps, ACT.Copy).then_inc(rows_read[h], 1)

            def ln2(t):
                i, h = t
                wait(act, mv2_ready[h], i + 1)
                nc.scalar.activation(lnv2[h][:, :], row[h][:, :, RSTD], ACT.Ln, bias=kc[:, K_EPS:K_EPS + 1])\
                    .then_inc(lnv2_ready[h], 1)
                wait(act, lnv2_ready[h], i + 1)
                nc.scalar.activation(row[h][:, :, RSTD], lnv2[h][:, :], ACT.Exp, scale=-0.5).then_inc(rstd2_ready[h], 1)

            def exp_k(t):
                i, h = t
                wait(act, num_ready[h], 2 * i)
                for g in range(G):
                    wait(act, kt_ready[h], 2 * i + g + 1)
                    nc.scalar.activation(ek[h][:, g, :], kt_ps[g][:, :], ACT.Exp).then_inc(ek_ready[h], 1)

            def invert(t, g):
                i, h = t
                wait(act, y_ready[h], 2 * i)
                wait(act, den_ready[h], 2 * i + g + 1)
                nc.scalar.activation(rd[h][:, g, :], den_ps[g][:, :], ACT.Ln).then_inc(lnd_ready[h], 1)
                wait(act, lnd_ready[h], 2 * i + g + 1)
                nc.scalar.activation(rd[h][:, g, :], rd[h][:, g, :], ACT.Exp, scale=-1.0).then_inc(rd_ready[h], 1)

            def start_y(t):
                i, h = t
                wait(act, v_in[h], 16 * (i + 1))
                wait(act, x2t_ready[h], 2 * i)
                nc.scalar.activation(yt[h][:, :, 0:NB:T], vt[h][:, :, 0:NB:T], ACT.Copy).then_inc(y0_ready[h], 1)

            def ln1(t):
                i, h = t
                wait(act, mv1_ready[h], i + 1)
                nc.scalar.activation(lnv1[h][:, :], mv1[h][:, :, 1], ACT.Ln, bias=kc[:, K_EPS:K_EPS + 1])\
                    .then_inc(lnv1_ready[h], 1)
                wait(act, lnv1_ready[h], i + 1)
                nc.scalar.activation(rstd1[h][:, :], lnv1[h][:, :], ACT.Exp, scale=-0.5).then_inc(rstd1_ready[h], 1)

            def normalise(t):
                i, h = t
                wait(act, x_in[h], 16 * (i + 1))
                wait(act, nmr1_ready[h], i + 1)
                wait(act, kt_ready[h], 2 * i)
                for j in range(JT):
                    last = nc.scalar.activation(xn[h][:, j, :], xr[h][:, j, :], ACT.Identity,
                                                bias=nmr1[h][:, j:j + 1], scale=rstd1[h][:, j:j + 1])
                last.then_inc(xn_ready[h], 1)

            def step(t, s):
                if active(s, 1):
                    exp_k(back(t, 1, 2))
                if active(s, 0):
                    ln1(t)
                if active(s, 2):
                    start_y(back(t, 2, 2))
                if active(s, 0):
                    normalise(t)
                if active(s, 2):
                    invert(back(t, 2, 2), 0)
                if active(s, 4):
                    ln2(back(t, 4, 2))
                if active(s, 2):
                    invert(back(t, 2, 2), 1)
                if active(s, 3):
                    evacuate(back(t, 3, 2))

            act.wait_ge(const_in, 16)
            run(act, step, 0, LOOP1, STEPS, 2)

            def evacuate3(t):
                i, k = t
                wait(act, ngt_tr[k], i + 1)
                wait(act, gu_ready[k], i)
                nc.scalar.activation(ngt[k][:, :, :], ngt_ps[k % 2][:, 0:G * P].rearrange("p (g n) -> p g n", g=G),
                                     ACT.Copy).then_inc(ngt_ready[k], 1)

            def silu(t):
                i, k = t
                wait(act, gu_ready[k], i + 1)
                wait(act, hh_ready[k], i)
                nc.scalar.activation(sg[k][:, :], gu_ps[k % 2][:, 0:I], ACT.Silu).then_inc(sg_ready[k], 1)
                wait(act, xg_in[k], 16 * (i + 1))
                nc.scalar.activation(th[k][:, :], rows_of(t)[:, GAP:GAP + 1], ACT.Tanh, scale=0.5).then_inc(th_ready[k], 1)

            def step3(t, s):
                if live(s, 2):
                    evacuate3(ahead(t, 2))
                if live(s, 1):
                    silu(ahead(t, 1))

            evacuate3((0, 0))
            evacuate3((0, 1))
            silu((0, 0))
            run(act, step3, 0, LOOP3, TILES, 4)

        @blk.tensor
        def _(pe):
            pe.wait_ge(const_in, 16)
            pe.wait_ge(rwt_tr, 1)
            for g in range(G):
                last = nc.tensor.transpose(rwt_ps[:, g, :], rwc[:, g * P:(g + 1) * P], kc[0:E, K_ID:K_ID + E])
            last.then_inc(rwt_tr, 1)
            pe.wait_ge(rwt_ready, 1)
            pe.wait_ge(diag_ready, 1)

            def rows(t):
                i, h = t
                pi, ph = back(t, 1, 2)
                wait(pe, x2t_ready[h], 2 * i + 2)
                wait(pe, logit_read[ph], pi + 1)
                for q in range(2):
                    if q == 0:
                        wait(pe, rows_read[ph], 2 * (pi + 1))
                    else:
                        wait(pe, rows_read[h], 2 * i + 1)
                    for j in range(2):
                        cols = slice((2 * q + j) * P, (2 * q + j + 1) * P)
                        for g in range(G):
                            last = nc.tensor.transpose(rows_ps[:, j, g * P:(g + 1) * P], x2t[h][:, g, cols], ident)
                    last.then_inc(rows_ready[h], 1)
                    if q == 1:
                        continue
                    for j in range(JT):
                        for g in range(G):
                            last = nc.tensor.matmul(logit_ps[:, j, :], x2t[h][:, g, j * P:(j + 1) * P], rwt[:, g, :],
                                                    start=(g == 0), stop=(g == G - 1))
                    last.then_inc(logit_ready[h], 1)

            def read_out(t):
                i, h = t
                pi, ph = back(t, 1, 2)
                for g in range(G):
                    wait(pe, scan_ready[h], 2 * i + g + 1)
                    for ps, now, state, free, done in (
                            (den_ps, ek, sk, lnd_ready, den_ready), (num_ps, ev, sv, y_ready, num_ready)):
                        wait(pe, free[ph], 2 * pi + g + 1)
                        nc.tensor.matmul(ps[g][:, :], diag[:, 1, g, :], now[h][:, g, :], start=True, stop=False)
                        nc.tensor.matmul(by_seq(ps[g][:, :])[:, :, 1:T], diag[:, 0, g, :],
                                         by_seq(state[h][:, g, :])[:, :, 0:T - 1],
                                         start=False, stop=True).then_inc(done[h], 1)

            def to_channels(t):
                i, h = t
                pi, ph = back(t, 1, 2)
                wait(pe, xn_ready[h], i + 1)
                for g in range(G):
                    wait(pe, ek_ready[ph], 2 * pi + g + 1)
                    for j in range(JT):
                        last = nc.tensor.transpose(kt_ps[g][:, j * P:(j + 1) * P], xn[h][:, j, g * P:(g + 1) * P], ident)
                    last.then_inc(kt_ready[h], 1)

            def step(t, s):
                if active(s, 2):
                    read_out(back(t, 2, 2))
                if active(s, 3):
                    rows(back(t, 3, 2))
                if active(s, 0):
                    to_channels(t)

            run(pe, step, 0, LOOP1, STEPS, 2)

            pe.wait_ge(hot_ready, 1)
            nc.tensor.matmul(bank[0][:, 0:E * NT], lt_b[:, :], hot[:, :, :].rearrange("p e i -> p (e i)"), start=True, stop=True)
            nc.tensor.matmul(bank[1][:, 0:E * NT], one_b[:, :], hot[:, :, :].rearrange("p e i -> p (e i)"),
                             start=True, stop=True).then_inc(rank_ready, 1)
            pe.wait_ge(num_hi_ready, 1)
            for n in range(NT):
                if n % 8 == 0:
                    pe.wait_ge(at_lo_ready, n // 8 + 1)
                last = nc.tensor.matmul(id_ps, at_lo[:, n, :], num_hi[:, n, :, :].rearrange("p a t -> p (a t)"),
                                        start=(n == 0), stop=(n == NT - 1))
            last.then_inc(id_ready, 1)

            pe.wait_ge(table_ready, 1)
            pe.wait_ge(wgu_in, 16)
            pe.wait_ge(wdn_in, 16)

            def transpose_x(t):
                i, k = t
                bi, bk = back(t, 2, 4)
                wait(pe, ng_ready[k], i + 1)
                wait(pe, ngt_ready[bk], bi + 1)
                for g in range(G):
                    last = nc.tensor.transpose(ngt_ps[k % 2][:, g * P:(g + 1) * P], ng[k][:, g * P:(g + 1) * P], ident)
                last.then_inc(ngt_tr[k], 1)

            def tile_expert(t):
                i, k = t
                return pe.value_load(expert[0:1, bass.ds(4 * i + k, 1)], min_val=0, max_val=E - 1)

            def gate_up(t):
                i, k = t
                bi, bk = back(t, 2, 4)
                e = tile_expert(t)
                wait(pe, ngt_ready[k], i + 1)
                wait(pe, hh_ready[bk], bi + 1)
                for g in range(G):
                    last = nc.tensor.matmul(gu_ps[k % 2][:, 0:2 * I], ngt[k][:, g, :],
                                            wgu[:, g, bass.ds(e, 1), :].rearrange("p o n -> p (o n)"),
                                            start=(g == 0), stop=(g == G - 1))
                last.then_inc(gu_ready[k], 1)

            def transpose_h(t):
                i, k = t
                bi, bk = back(t, 2, 4)
                wait(pe, hh_ready[k], i + 1)
                wait(pe, hht_ready[bk], bi + 1)
                for a in range(2):
                    last = nc.tensor.transpose(hht_ps[k % 2][0:IH, a * P:(a + 1) * P], hh[k][:, a * IH:(a + 1) * IH], ident)
                last.then_inc(hht_tr[k], 1)

            def down(t):
                i, k = t
                bi, bk = back(t, 2, 4)
                e = tile_expert(t)
                wait(pe, hht_ready[k], i + 1)
                wait(pe, ob_ready[bk], bi + 1)
                for a in range(2):
                    last = nc.tensor.matmul(o_ps[k % 2][:, 0:C], hht[k][:, a, :],
                                            wdn[:, a, bass.ds(e, 1), :].rearrange("p o n -> p (o n)"),
                                            start=(a == 0), stop=(a == 1))
                last.then_inc(o_ready[k], 1)

            def step3(t, s):
                if live(s, 2):
                    transpose_x(ahead(t, 2))
                transpose_h(t)
                if live(s, 1):
                    gate_up(ahead(t, 1))
                down(t)

            transpose_x((0, 0))
            transpose_x((0, 1))
            gate_up((0, 0))
            run(pe, step3, 0, LOOP3, TILES, 4)

        @blk.vector
        def _(dve):
            vec = nc.vector
            dve.wait_ge(wu_in, 32)
            vec.tensor_scalar_max(bonus[:, 0, :], wu[:, 1, :], 0.0)
            vec.tensor_scalar_min(bonus[:, 1, :], wu[:, 1, :], 0.0).then_inc(setup_v, 1)
            dve.wait_ge(rw_in, 16)
            vec.reduce_sum(rsum[:, :], rw[:, :], AX.X).then_inc(setup_v, 1)
            vec.memset(decay[:, :, :], 0.0)
            vec.memset(same_e[:, :, :], 1.0)
            vec.memset(one_b[:, :], 1.0)
            vec.memset(ones8[:, :], 1.0)
            vec.memset(row[0][:, :, GAP:ROW], 0.0)
            vec.memset(row[1][:, :, GAP:ROW], 0.0).then_inc(setup_v, 1)
            dve.wait_ge(setup_v, 3)
            vec.tensor_scalar_mul(rmean[:, :], rsum[:, :], 1.0 / C).then_inc(setup_v, 1)
            vec.memset(same_e[:, :, 0], 0.0)
            dve.wait_ge(setup_v, 4)
            vec.tensor_scalar_sub(rwc[:, :], rw[:, :], rmean[:, 0:1]).then_inc(rwt_tr, 1)
            dve.wait_ge(const_in, 16)
            vec.tensor_copy(lt_b[:, :], kc[:, K_LT:K_LT + P])
            vec.tensor_copy(iota_b[:, :], kc[:, K_IOTA:K_IOTA + P])
            dve.wait_ge(ab_ready, 1)
            for g in range(G):
                vec.tensor_copy(by_seq(decay[:, g, :])[:, :, 1:T],
                                decay1[:, g:g + 1].unsqueeze(2).to_broadcast([P, SEQ, T - 1]))
                for n in range(2):
                    last = vec.tensor_scalar_mul(diag[:, n, g, :], ident, ab[:, n, g:g + 1])
            last.then_inc(diag_ready, 1)
            dve.wait_ge(diag_ready, 1)
            dve.wait_ge(rwt_tr, 2)
            vec.tensor_copy(rwt[:, :, :], rwt_ps).then_inc(rwt_ready, 1)

            def stats1(t):
                i, h = t
                wait(dve, x_in[h], 16 * (i + 1))
                wait(dve, xn_ready[h], i)
                for j in range(JT):
                    last = vec.bn_stats(six1[h][:, j, :], xr[h][:, j, :])
                last.then_inc(six1_ready[h], 1)
                wait_apart(dve, six1_ready[h], i + 1)
                for j in range(JT):
                    last = vec.bn_aggr(mv1[h][:, j, :], six1[h][:, j, :])
                last.then_inc(mv1_ready[h], 1)

            def shift1(t):
                i, h = t
                wait(dve, rstd1_ready[h], i + 1)
                vec.scalar_tensor_tensor(out=nmr1[h][:, :], in0=mv1[h][:, :, 0], scalar=-1.0, in1=rstd1[h][:, :],
                                         op0=ALU.mult, op1=ALU.mult).then_inc(nmr1_ready[h], 1)

            def scans(t):
                i, h = t
                wait(dve, num_ready[h], 2 * i)
                for g in range(G):
                    for state, data, ready in ((sk, ek, ek_ready), (sv, ev, ev_ready)):
                        wait(dve, ready[h], 2 * i + g + 1)
                        last = vec.tensor_tensor_scan(state[h][:, g, :], decay[:, g, :], data[h][:, g, :], 0.0,
                                                      ALU.mult, ALU.add)
                    last.then_inc(scan_ready[h], 1)

            def divide(t):
                i, h = t
                wait(dve, x2t_ready[h], 2 * i)
                for g in range(G):
                    wait(dve, num_ready[h], 2 * i + g + 1)
                    wait(dve, rd_ready[h], 2 * i + g + 1)
                    vec.tensor_tensor(by_seq(yt[h][:, g, :])[:, :, 1:T], by_seq(num_ps[g][:, :])[:, :, 1:T],
                                      by_seq(rd[h][:, g, :])[:, :, 1:T], ALU.mult).then_inc(y_ready[h], 1)

            def stats2(t):
                i, h = t
                wait(dve, rows_out[h], 16 * i)
                wait(dve, logit_ready[h], i + 1)
                vec.tensor_copy(logit[:, bass.ds((2 * i + h) * JT, JT), :], logit_ps)
                for j in range(JT):
                    last = vec.max(top[h][:, j, :], logit_ps[:, j, :])
                last.then_inc(logit_read[h], 1)
                for j in range(JT):
                    if j % 2 == 0:
                        wait(dve, rows_read[h], 2 * i + j // 2 + 1)
                    last = vec.bn_stats(six2[h][:, j, :], row[h][:, j, 0:C])
                last.then_inc(six2_ready[h], 1)
                wait(dve, logit_read[h], i + 1)
                vec.tensor_sub(gap[h][:, :], top[h][:, :, 0], top[h][:, :, 1]).then_inc(gap_ready[h], 1)
                wait_apart(dve, six2_ready[h], i + 1)
                for j in range(JT):
                    last = vec.bn_aggr(row[h][:, j, MEAN:RSTD + 1], six2[h][:, j, :])
                last.then_inc(mv2_ready[h], 1)

            def scale_gap(t):
                i, h = t
                wait(dve, rstd2_ready[h], i + 1)
                wait(dve, gap_ready[h], i + 1)
                vec.tensor_tensor(row[h][:, :, GAP], gap[h][:, :], row[h][:, :, RSTD], ALU.mult)\
                    .then_inc(row_ready[h], 1)

            def step(t, s):
                if active(s, 0):
                    stats1(t)
                if active(s, 4):
                    stats2(back(t, 4, 2))
                if active(s, 0):
                    shift1(t)
                if active(s, 1):
                    scans(back(t, 1, 2))
                if active(s, 4):
                    scale_gap(back(t, 4, 2))
                if active(s, 2):
                    divide(back(t, 2, 2))

            run(dve, step, 0, LOOP1, STEPS, 2)

            done = [0]

            def link(ins):
                done[0] += 1
                ins.then_inc(route_v, 1)
                dve.wait_ge(route_v, done[0])

            wide = [P, NT, E]
            for h in range(2):
                dve.wait_ge(row_ready[h], BLOCKS // 2)
            link(vec.tensor_reduce(best[:, :], logit[:, :, :], AX.X, ALU.max))
            link(vec.tensor_tensor(is_best[:, :, :], logit[:, :, :], best[:, :].unsqueeze(2).to_broadcast(wide), ALU.is_ge))
            e8 = kc[:, K_E8:K_E8 + E].unsqueeze(1).to_broadcast(wide)
            link(vec.tensor_tensor(cand[:, :, :], is_best[:, :, :], e8, ALU.mult))
            link(vec.tensor_reduce(first[:, :], cand[:, :, :], AX.X, ALU.min))
            vec.tensor_tensor(hot[:, :, :].rearrange("p e i -> p i e"), e8,
                              first[:, :].unsqueeze(2).to_broadcast(wide), ALU.is_equal).then_inc(hot_ready, 1)
            dve.wait_ge(rank_ready, 1)
            dve.wait_ge(hot_ready, 1)
            link(vec.tensor_tensor_scan(upto[:, :, :].rearrange("p e i -> p (e i)"), same_e[:, :, :].rearrange("p e i -> p (e i)"),
                                        bank[1][:, 0:E * NT], 0.0, ALU.mult, ALU.add))
            link(vec.tensor_scalar_add(cnt_i[:, :], upto[:, :, NT - 1], float(P - 1)))
            link(vec.tensor_single_scalar(nt_i[:, :], cnt_i[:, :], 7, ALU.arith_shift_right))
            link(vec.tensor_copy(nt_f[:, :], nt_i[:, :]))
            link(vec.tensor_tensor_scan(end_f[:, :], ones8[:, :], nt_f[:, :], 0.0, ALU.mult, ALU.add))
            vec.tensor_tensor(before[:, :, :], upto[:, :, :], tot_ps, ALU.subtract)
            link(vec.tensor_sub(base[:, :], end_f[:, :], nt_f[:, :]))
            link(vec.tensor_tensor(slot3[:, :, :], before[:, :, :], rank_ps, ALU.add))
            link(vec.scalar_tensor_tensor(out=before[:, :, :], in0=base[:, :].unsqueeze(2).to_broadcast([P, E, NT]),
                                          scalar=float(P), in1=slot3[:, :, :], op0=ALU.mult, op1=ALU.add))
            link(vec.tensor_tensor(slot3[:, :, :], before[:, :, :], hot[:, :, :], ALU.mult))
            link(vec.reduce_sum(slot[:, :], slot3[:, :, :].rearrange("p e i -> p i e"), AX.X))
            link(vec.tensor_copy(slot_i[:, :], slot[:, :]))
            vec.tensor_single_scalar(lo_i[:, :], slot_i[:, :], P - 1, ALU.bitwise_and)
            link(vec.tensor_single_scalar(hi_i[:, :], slot_i[:, :], 7, ALU.arith_shift_right))
            vec.tensor_copy(lo_f[:, :], lo_i[:, :])
            link(vec.tensor_copy(hi_f[:, :], hi_i[:, :]))
            per_tile = [P, NT, TILES]
            link(vec.tensor_tensor(at_hi[:, :, :], kc[:, K_IOTA:K_IOTA + TILES].unsqueeze(1).to_broadcast(per_tile),
                                   hi_f[:, :].unsqueeze(2).to_broadcast(per_tile), ALU.is_equal))
            vec.tensor_tensor(num_hi[:, :, 0, :], at_hi[:, :, :],
                              kc[:, K_TILE:K_TILE + NT].unsqueeze(2).to_broadcast(per_tile), ALU.mult)
            vec.tensor_scalar_mul(num_hi[:, :, 1, :], at_hi[:, :, :], kc[:, K_P:K_P + 1]).then_inc(num_hi_ready, 1)
            for n in range(NT):
                last = vec.tensor_scalar(at_lo[:, n, :], iota_b[:, :], lo_f[:, n:n + 1], None, ALU.is_equal)
                if n % 8 == 7:
                    last.then_inc(at_lo_ready, 1)
            shape = [1, TILES, E]
            link(vec.tensor_tensor(past[:, :, :], kc[0:1, K_IOTA:K_IOTA + TILES].unsqueeze(2).to_broadcast(shape),
                                   end_f[0:1, :].unsqueeze(1).to_broadcast(shape), ALU.is_ge))
            link(vec.reduce_sum(expert_f[:, :], past[:, :, 0:E - 1], AX.X))
            link(vec.tensor_copy(expert[:, :], expert_f[:, :]))
            dve.wait_ge(id_ready, 1)
            link(vec.tensor_scalar(id_hi[:, :], id_ps[:, 0:TILES], float(P), float(PAD_ID), ALU.mult, ALU.add))
            link(vec.tensor_tensor(id_f[:, :], id_hi[:, :], id_ps[:, TILES:2 * TILES], ALU.add))
            link(vec.tensor_copy(put_id[:, :], id_f[:, :]))
            vec.tensor_single_scalar(get_id[:, :], put_id[:, :], TOK - 1, ALU.bitwise_and).then_inc(table_ready, 1)

            def normalise3(t):
                i, k = t
                wait(dve, xg_in[k], 16 * (i + 1))
                wait(dve, ngt_tr[k], i)
                xt_ = rows_of(t)
                vec.tensor_scalar(ng[k][:, :], xt_[:, 0:C], xt_[:, MEAN:MEAN + 1], xt_[:, RSTD:RSTD + 1],
                                  ALU.subtract, ALU.mult).then_inc(ng_ready[k], 1)

            def hidden(t):
                i, k = t
                wait(dve, sg_ready[k], i + 1)
                wait(dve, hht_tr[k], i)
                vec.tensor_tensor(hh[k][:, :], gu_ps[k % 2][:, I:2 * I], sg[k][:, :], ALU.mult).then_inc(hh_ready[k], 1)
                wait(dve, th_ready[k], i + 1)
                vec.tensor_scalar(wt[k][:, :], th[k][:, :], 0.5, 0.5, ALU.mult, ALU.add).then_inc(wt_ready[k], 1)

            def evacuate_h(t):
                i, k = t
                wait(dve, hht_tr[k], i + 1)
                wait(dve, o_ready[k], i)
                vec.tensor_copy(hht[k][:, :, :], hht_ps[k % 2][0:IH, 0:2 * P].rearrange("p (a n) -> p a n", a=2))\
                    .then_inc(hht_ready[k], 1)

            def finish(t):
                i, k = t
                wait(dve, o_ready[k], i + 1)
                wait(dve, wt_ready[k], i + 1)
                wait(dve, put_out[k], 16 * i)
                vec.scalar_tensor_tensor(out=ob[k][:, :], in0=o_ps[k % 2][:, 0:C], scalar=wt[k][:, 0:1],
                                         in1=rows_of(t)[:, 0:C], op0=ALU.mult, op1=ALU.add).then_inc(ob_ready[k], 1)

            def step3(t, s):
                if live(s, 3):
                    normalise3(ahead(t, 3))
                evacuate_h(t)
                if live(s, 1):
                    hidden(ahead(t, 1))
                finish(t)

            for s in range(3):
                normalise3((0, s))
            hidden((0, 0))
            run(dve, step3, 0, LOOP3, TILES, 4)


def kernel(x, ctx_2048, L0_xattn_w, L0_xattn_u, L0_ffn_router_w, L0_ffn_gate_w, L0_ffn_up_w, L0_ffn_down_w):
    import concourse.bacc as bacc
    from concourse.bass_utils import run_bass_kernel_spmd

    def dense(a):
        return np.ascontiguousarray(a)

    x, c = np.asarray(x).reshape(TOK, C), np.asarray(ctx_2048).reshape(TOK, C)
    gate_up = np.concatenate([np.asarray(L0_ffn_gate_w), np.asarray(L0_ffn_up_w)], axis=1)
    arrays = {
        "x": dense(x),
        "x_t": dense(x.T),
        "ctx_t": dense(c.T),
        "w": dense(np.asarray(L0_xattn_w).reshape(G, P).T),
        "u": dense(np.asarray(L0_xattn_u).reshape(G, P).T),
        "router": dense(L0_ffn_router_w),
        "gate_up_t": dense(gate_up.transpose(2, 0, 1)),
        "down_t": dense(np.asarray(L0_ffn_down_w).transpose(2, 0, 1)),
        "consts": constants(),
    }
    nc = bacc.Bacc("TRN2", target_bir_lowering=False, num_devices=1)
    args = [nc.dram_tensor(n, a.shape, mybir.dt.from_np(a.dtype), kind="ExternalInput").ap() for n, a in arrays.items()]
    out = nc.dram_tensor("out", (TOK, C), F32, kind="ExternalOutput").ap()
    build(nc, *args, out)
    r = run_bass_kernel_spmd(nc, [arrays], core_ids=[0])
    return r.results[0]["out"].reshape(B, T, C)
```

```python
from contextlib import ExitStack

import numpy as np
import concourse.bass as bass
from concourse import mybir

P = 128
B, T, C = 64, 64, 256
TOK = B * T
G = C // P
NB = 512
BLOCKS = TOK // NB
JT = NB // P
SEQ = NB // T
NT = TOK // P
E, I = 8, 176
IH = I // 2
BITS = 3
TILES = (TOK + E * (P - 1)) // P
ROUNDS = (TILES + 3) // 4
ROW = C + 4
MEAN, RSTD, GAP = C, C + 1, C + 2
PAD_ID = 2 * TOK
EPS = 1e-5
U_MAX = 56.0

F32, BF16, I32, U32 = mybir.dt.float32, mybir.dt.bfloat16, mybir.dt.int32, mybir.dt.uint32
ALU = mybir.AluOpType
ACT = mybir.ActivationFunctionType
AX = mybir.AxisListType

K_ID, K_LT, K_IOTA, K_E8, K_TILE, K_P, K_EPS, K_POW = 0, 128, 256, 384, 392, 424, 425, 426
K_ALL = 430


def constants():
    k = np.zeros((P, K_ALL), np.float32)
    p = np.arange(P)
    k[:, K_ID:K_ID + P] = np.eye(P)
    k[:, K_LT:K_LT + P] = p[:, None] < p[None, :]
    k[:, K_IOTA:K_IOTA + P] = p[None, :]
    k[:, K_E8:K_E8 + E] = np.arange(E) - E
    k[:, K_TILE:K_TILE + NT] = np.arange(NT) - PAD_ID // P
    k[:, K_P] = p
    k[:, K_EPS] = EPS
    k[:, K_POW:K_POW + 4] = 8.0 ** np.arange(4)
    return k


def build(nc, x, x_t, ctx_t, w, u, router, gate_up_t, down_t, consts, out):
    ctx = ExitStack()
    with ctx:
        def sb(name, shape, dt=F32):
            return ctx.enter_context(nc.sbuf_tensor(name, shape, dt))

        def sem(name):
            return ctx.enter_context(nc.semaphore(name))

        def sems(name, n):
            return [sem(f"{name}{k}") for k in range(n)]

        def wait(eng, s, value):
            if not (isinstance(value, int) and value <= 0):
                eng.wait_ge(s, value)

        scratch = nc.dram_tensor("x2_rows", (TOK, ROW), F32, kind="Internal").ap()

        kc = sb("kc", [P, K_ALL])
        ident = kc[:, K_ID:K_ID + P]
        wgu = sb("wgu", [P, G, E, 2 * I])
        wdn = sb("wdn", [IH, 2, E, C])
        wu = sb("wu", [P, 2, G])
        bonus = sb("bonus", [P, G])
        down_by = sb("down_by", [P, G])
        exp_w = sb("exp_w", [P, G])
        exp_u = sb("exp_u", [P, G])
        shrink = sb("shrink", [P, G])
        diag = sb("diag", [P, G, P])
        rw = sb("rw", [E, C])
        rsum = sb("rsum", [E, 1])
        rmean = sb("rmean", [E, 1])
        rwc = sb("rwc", [E, C])
        rwt = sb("rwt", [P, G, E])

        def two(name, shape, dt=F32):
            return [sb(f"{name}{h}", shape, dt) for h in range(2)]

        pool_w = JT * C
        assert TILES * ROW <= 10 * pool_w and G * NB == pool_w
        shared = sb("shared", [P, 10 * pool_w])
        xg = shared[:, 0:TILES * ROW].rearrange("p (n c) -> p n c", c=ROW)

        def pair(n, inner):
            return [shared[:, k * pool_w:(k + 1) * pool_w].rearrange("p (a b) -> p a b", b=inner)
                    for k in (2 * n, 2 * n + 1)]

        xr = pair(0, C)
        xn = pair(1, C)
        xt = pair(2, NB)
        vt = pair(3, NB)
        ek = pair(4, NB)
        eb = two("eb", [P, G, NB])
        ev = two("ev", [P, G, NB])
        sk = two("sk", [P, G, NB])
        sv = two("sv", [P, G, NB])
        decay = two("decay", [P, NB])
        yt = two("yt", [P, G, NB])
        x2t = two("x2t", [P, G, NB])
        row = two("row", [P, JT, ROW])
        six1 = two("six1", [P, JT, 6])
        mv1 = two("mv1", [P, JT, 2])
        lnv1 = two("lnv1", [P, JT])
        rstd1 = two("rstd1", [P, JT])
        nmr1 = two("nmr1", [P, JT])
        six2 = two("six2", [P, JT, 6])
        lnv2 = two("lnv2", [P, JT])
        top = two("top", [P, JT, 8])
        gap = two("gap", [P, JT])
        logit = sb("logit", [P, NT, E])

        best = sb("best", [P, NT])
        is_best = sb("is_best", [P, NT, E])
        cand = sb("cand", [P, NT, E])
        first = sb("first", [P, NT])
        hot = sb("hot", [P, E, NT], BF16)
        lt_b = sb("lt_b", [P, P], BF16)
        one_b = sb("one_b", [P, P], BF16)
        iota_b = sb("iota_b", [P, P], BF16)
        same_e = sb("same_e", [P, E, NT])
        ones8 = sb("ones8", [P, E])
        upto = sb("upto", [P, E, NT])
        before = sb("before", [P, E, NT])
        slot3 = sb("slot3", [P, E, NT])
        cnt_i = sb("cnt_i", [P, E], I32)
        nt_i = sb("nt_i", [P, E], I32)
        nt_f = sb("nt_f", [P, E])
        end_f = sb("end_f", [P, E])
        base = sb("base", [P, E])
        slot = sb("slot", [P, NT])
        slot_i = sb("slot_i", [P, NT], I32)
        lo_i = sb("lo_i", [P, NT], I32)
        hi_i = sb("hi_i", [P, NT], I32)
        lo_f = sb("lo_f", [P, NT])
        hi_f = sb("hi_f", [P, NT])
        at_lo = sb("at_lo", [P, NT, P], BF16)
        at_hi = sb("at_hi", [P, NT, TILES])
        num_hi = sb("num_hi", [P, NT, 2, TILES], BF16)
        id_hi = sb("id_hi", [P, TILES])
        id_f = sb("id_f", [P, TILES])
        put_id = sb("put_id", [P, TILES], I32)
        get_id = sb("get_id", [P, TILES], I32)
        past = sb("past", [1, TILES, E])
        expert_f = sb("expert_f", [1, 4 * ROUNDS + 4])
        shifted = sb("shifted", [1, ROUNDS, 4])
        word_f = sb("word_f", [1, ROUNDS])
        word = sb("word", [1, ROUNDS], I32)

        def four(name, shape, dt=F32):
            return [sb(f"{name}{k}", shape, dt) for k in range(4)]

        ng = four("ng", [P, C])
        ngt = four("ngt", [P, G, P])
        sg = four("sg", [P, I])
        hh = four("hh", [P, I])
        hht = four("hht", [IH, 2, P])
        th = four("th", [P, 1])
        wt = four("wt", [P, 1])
        ob = four("ob", [P, C])

        bank = [ctx.enter_context(nc.psum_tensor(f"bank{n}", [P, 512], F32)) for n in range(8)]
        kt_ps, num_ps = bank[0:2], bank[4:6]
        rows_ps = [bank[n][:, :].rearrange("p (j c) -> p j c", j=2) for n in (2, 6)]
        logit_ps = bank[7][:, 0:JT * E].rearrange("p (j e) -> p j e", e=E)
        rwt_ps = bank[7][:, 0:G * E].rearrange("p (g e) -> p g e", e=E)
        rank_ps = bank[0][:, 0:E * NT].rearrange("p (e i) -> p e i", e=E)
        tot_ps = bank[1][:, 0:E * NT].rearrange("p (e i) -> p e i", e=E)
        id_ps = bank[2][:, 0:2 * TILES]
        ngt_ps, gu_ps, hht_ps, o_ps = bank[0:2], bank[2:4], bank[4:6], bank[6:8]

        const_in, wu_in, rw_in, wgu_in, wdn_in = (sem(n) for n in (
            "const_in", "wu_in", "rw_in", "wgu_in", "wdn_in"))
        setup_v, exp_wu_ready, diag_ready, rwt_tr, rwt_ready = (sem(n) for n in (
            "setup_v", "exp_wu_ready", "diag_ready", "rwt_tr", "rwt_ready"))
        x_in, xt_in, v_in, rows_out = (sems(n, 2) for n in ("x_in", "xt_in", "v_in", "rows_out"))
        six1_ready, mv1_ready, lnv1_ready, rstd1_ready, nmr1_ready, xn_ready = (sems(n, 2) for n in (
            "six1_ready", "mv1_ready", "lnv1_ready", "rstd1_ready", "nmr1_ready", "xn_ready"))
        kt_ready, ek_ready, eb_ready, ev_ready, sv_ready, sk_ready = (sems(n, 2) for n in (
            "kt_ready", "ek_ready", "eb_ready", "ev_ready", "sv_ready", "sk_ready"))
        den_ready, num_ready, lnd_ready, rd_ready, y0_ready, y_ready, x2t_ready = (sems(n, 2) for n in (
            "den_ready", "num_ready", "lnd_ready", "rd_ready", "y0_ready", "y_ready", "x2t_ready"))
        rows_ready, rows_read, logit_ready, logit_read = (sems(n, 2) for n in (
            "rows_ready", "rows_read", "logit_ready", "logit_read"))
        six2_ready, mv2_ready, lnv2_ready, rstd2_ready, gap_ready, row_ready = (sems(n, 2) for n in (
            "six2_ready", "mv2_ready", "lnv2_ready", "rstd2_ready", "gap_ready", "row_ready"))
        route_v, hot_ready, rank_ready, at_lo_ready, num_hi_ready, id_ready, table_ready = (sem(n) for n in (
            "route_v", "hot_ready", "rank_ready", "at_lo_ready", "num_hi_ready", "id_ready", "table_ready"))
        xg_in, ng_ready, ngt_tr, ngt_ready, gu_ready, sg_ready, hh_ready = (sems(n, 4) for n in (
            "xg_in", "ng_ready", "ngt_tr", "ngt_ready", "gu_ready", "sg_ready", "hh_ready"))
        hht_tr, hht_ready, th_ready, wt_ready, o_ready, ob_ready, put_out = (sems(n, 4) for n in (
            "hht_tr", "hht_ready", "th_ready", "wt_ready", "o_ready", "ob_ready", "put_out"))

        def wait_apart(eng, s, value):
            eng.wait_ge(const_in, 16)
            wait(eng, s, value)

        def back(t, n, slots):
            i, k = t
            k -= n
            while k < 0:
                k += slots
                i = i - 1
            return i, k

        def rows_of(t):
            i, k = t
            return xg[:, bass.ds(4 * i + k, 1), :].rearrange("p o c -> p (o c)")

        def ahead2(t):
            i, h = t
            return (i, 1) if h == 0 else (i + 1, 0)

        def ahead(t, n):
            i, k = t
            return (i, k + n) if k + n < 4 else (i + 1, k + n - 4)

        def run(eng, step, first, loop, last, slots):
            if loop is None:
                for s in range(first, last):
                    step((s // slots, s % slots), s)
                return
            for s in range(first, loop[0] * slots):
                step((s // slots, s % slots), s)
            with eng.Fori(loop[0], loop[1]) as i:
                for k in range(slots):
                    step((i, k), None)
            for s in range(loop[1] * slots, last):
                step((s // slots, s % slots), s)

        LAG = 4
        STEPS = BLOCKS + LAG
        LOOP1 = None
        LOOP3 = (1, TILES // 4)

        def active(s, lag):
            return s is None or 0 <= s - lag < BLOCKS

        def live(s, ahead):
            return s is None or 0 <= s + ahead < TILES

        x_v = x.rearrange("(b j p) c -> p b j c", j=JT, p=P)
        xt_v = x_t.rearrange("(g p) (b n) -> p b g n", p=P, n=NB)
        ct_v = ctx_t.rearrange("(g p) (b n) -> p b g n", p=P, n=NB)
        sc_v = scratch.rearrange("(b j p) c -> p b j c", j=JT, p=P)

        def by_seq(a):
            return a.rearrange("p (s t) -> p s t", t=T)

        blk = ctx.enter_context(nc.Block())

        @blk.sync
        def _(sp):
            def load_rows(t):
                i, h = t
                wait(sp, xn_ready[h], i)
                sp.dma_start(xr[h][:, :, :], x_v[:, 2 * i + h]).then_inc(x_in[h], 16)

            def load_ctx(t):
                i, h = t
                wait(sp, ev_ready[h], 2 * i)
                wait(sp, y0_ready[h], i)
                sp.dma_start(vt[h][:, :, :], ct_v[:, 2 * i + h]).then_inc(v_in[h], 16)

            def load_columns(t):
                i, h = t
                wait(sp, x2t_ready[h], 2 * i)
                sp.dma_start(xt[h][:, :, :], xt_v[:, 2 * i + h]).then_inc(xt_in[h], 16)

            def load_expert(e):
                sp.dma_start(wgu[:, :, e, :], gate_up_t[:, e, :].rearrange("(g p) n -> p g n", p=P)).then_inc(wgu_in, 16)
                sp.dma_start(wdn[:, :, e, :], down_t[:, e, :].rearrange("(a p) n -> p a n", p=IH)).then_inc(wdn_in, 16)

            def store(t):
                i, h = t
                wait(sp, row_ready[h], i + 1)
                sp.dma_start(sc_v[:, 2 * i + h], row[h][:, :, :]).then_inc(rows_out[h], 16)

            def step(t, s):
                if active(s, -1):
                    load_rows(ahead2(t))
                if active(s, 1):
                    load_columns(back(t, 1, 2))
                if active(s, 0):
                    load_ctx(t)
                if active(s, 2):
                    load_expert(s - 2)
                if active(s, LAG):
                    store(back(t, LAG, 2))

            load_rows((0, 0))
            run(sp, step, 0, LOOP1, STEPS, 2)
            for k in range(4):
                wait(sp, put_out[k], 16 * len(range(k, TILES, 4)))

        @blk.gpsimd
        def _(pool):
            def weigh(t):
                i, h = t
                wait(pool, v_in[h], 16 * (i + 1))
                wait(pool, num_ready[h], 2 * i)
                for g in range(G):
                    wait(pool, ek_ready[h], 2 * i + g + 1)
                    nc.gpsimd.tensor_tensor(ev[h][:, g, :], ek[h][:, g, :], vt[h][:, g, :],
                                            ALU.mult).then_inc(ev_ready[h], 1)

            def residual(t):
                i, h = t
                wait(pool, xt_in[h], 16 * (i + 1))
                wait(pool, y0_ready[h], i + 1)
                wait(pool, rows_ready[h], 2 * i)
                wait(pool, logit_ready[h], i)
                for g in range(G):
                    wait(pool, y_ready[h], 2 * i + g + 1)
                    nc.gpsimd.tensor_tensor(x2t[h][:, g, :], yt[h][:, g, :], xt[h][:, g, :],
                                            ALU.add).then_inc(x2t_ready[h], 1)

            def denominator(t):
                i, h = t
                for g in range(G):
                    wait(pool, eb_ready[h], 2 * i + g + 1)
                    wait(pool, sk_ready[h], 2 * i + g + 1)
                    now = by_seq(eb[h][:, g, :])[:, :, 1:T]
                    nc.gpsimd.tensor_tensor(now, now, by_seq(sk[h][:, g, :])[:, :, 0:T - 1], ALU.add)\
                        .then_inc(den_ready[h], 1)

            def step(t, s):
                if active(s, 2):
                    denominator(back(t, 2, 2))
                if active(s, 1):
                    weigh(back(t, 1, 2))
                if active(s, 2):
                    residual(back(t, 2, 2))

            run(pool, step, 0, LOOP1, STEPS, 2)

            for h in range(2):
                wait(pool, rows_out[h], 16 * (BLOCKS // 2))
            pool.wait_ge(table_ready, 1)

            def gather(n):
                wait(pool, ng_ready[n % 4], n // 4)
                pool.indirect_dma_start(
                    out=xg[:, n, :], out_offset=None, in_=scratch,
                    in_offset=bass.IndirectOffsetOnAxis(ap=get_id[:, n:n + 1], axis=0)).then_inc(xg_in[n % 4], 16)

            def scatter(n):
                wait(pool, ob_ready[n % 4], n // 4 + 1)
                pool.indirect_dma_start(
                    out=out, out_offset=bass.IndirectOffsetOnAxis(ap=put_id[:, n:n + 1], axis=0),
                    in_=ob[n % 4][:, :], in_offset=None, bounds_check=TOK - 1, oob_is_err=False)\
                    .then_inc(put_out[n % 4], 16)

            LEAD = 7
            for n in range(LEAD):
                gather(n)
            for n in range(TILES):
                if n + LEAD < TILES:
                    gather(n + LEAD)
                scatter(n)

        @blk.scalar
        def _(act):
            act.dma_start(wu[:, 0, :], w).then_inc(wu_in, 16)
            act.dma_start(wu[:, 1, :], u).then_inc(wu_in, 16)
            act.dma_start(kc[:, :], consts).then_inc(const_in, 16)
            act.dma_start(rw[:, :], router).then_inc(rw_in, 16)
            nc.scalar.preload_act_table_set("natural_log_exp_and_others")
            act.wait_ge(wu_in, 32)
            act.wait_ge(setup_v, 2)
            nc.scalar.activation(exp_w[:, :], wu[:, 0, :], ACT.Exp)
            nc.scalar.activation(shrink[:, :], down_by[:, :], ACT.Exp)
            nc.scalar.activation(exp_u[:, :], bonus[:, :], ACT.Exp).then_inc(exp_wu_ready, 1)

            def evacuate(t):
                i, h = t
                wait(act, rows_out[h], 16 * i)
                for q in range(2):
                    wait(act, rows_ready[h], 2 * i + q + 1)
                    nc.scalar.activation(row[h][:, 2 * q:2 * q + 2, 0:C], rows_ps[q], ACT.Copy).then_inc(rows_read[h], 1)

            def ln2(t):
                i, h = t
                wait(act, mv2_ready[h], i + 1)
                nc.scalar.activation(lnv2[h][:, :], row[h][:, :, RSTD], ACT.Ln, bias=kc[:, K_EPS:K_EPS + 1])\
                    .then_inc(lnv2_ready[h], 1)
                wait(act, lnv2_ready[h], i + 1)
                nc.scalar.activation(row[h][:, :, RSTD], lnv2[h][:, :], ACT.Exp, scale=-0.5).then_inc(rstd2_ready[h], 1)

            def exp_k(t):
                i, h = t
                wait(act, ev_ready[h], 2 * i)
                wait(act, sk_ready[h], 2 * i)
                for g in range(G):
                    wait(act, kt_ready[h], 2 * i + g + 1)
                    nc.scalar.activation(ek[h][:, g, :], kt_ps[g][:, :], ACT.Exp).then_inc(ek_ready[h], 1)

            def exp_ku(t):
                i, h = t
                wait(act, y_ready[h], 2 * i)
                for g in range(G):
                    nc.scalar.activation(eb[h][:, g, :], kt_ps[g][:, :], ACT.Exp, bias=bonus[:, g:g + 1])\
                        .then_inc(eb_ready[h], 1)

            def invert(t, g):
                i, h = t
                wait(act, den_ready[h], 2 * i + g + 1)
                now = by_seq(eb[h][:, g, :])[:, :, 1:T]
                nc.scalar.activation(now, now, ACT.Ln, scale=shrink[:, g:g + 1]).then_inc(lnd_ready[h], 1)
                wait(act, lnd_ready[h], 2 * i + g + 1)
                nc.scalar.activation(now, now, ACT.Exp, bias=down_by[:, g:g + 1], scale=-1.0).then_inc(rd_ready[h], 1)

            def start_y(t):
                i, h = t
                wait(act, v_in[h], 16 * (i + 1))
                wait(act, x2t_ready[h], 2 * i)
                nc.scalar.activation(yt[h][:, :, 0:NB:T], vt[h][:, :, 0:NB:T], ACT.Copy).then_inc(y0_ready[h], 1)

            def ln1(t):
                i, h = t
                wait(act, mv1_ready[h], i + 1)
                nc.scalar.activation(lnv1[h][:, :], mv1[h][:, :, 1], ACT.Ln, bias=kc[:, K_EPS:K_EPS + 1])\
                    .then_inc(lnv1_ready[h], 1)
                wait(act, lnv1_ready[h], i + 1)
                nc.scalar.activation(rstd1[h][:, :], lnv1[h][:, :], ACT.Exp, scale=-0.5).then_inc(rstd1_ready[h], 1)

            def normalise(t):
                i, h = t
                wait(act, x_in[h], 16 * (i + 1))
                wait(act, nmr1_ready[h], i + 1)
                wait(act, kt_ready[h], 2 * i)
                for j in range(JT):
                    last = nc.scalar.activation(xn[h][:, j, :], xr[h][:, j, :], ACT.Identity,
                                                bias=nmr1[h][:, j:j + 1], scale=rstd1[h][:, j:j + 1])
                last.then_inc(xn_ready[h], 1)

            def step(t, s):
                if active(s, 1):
                    exp_k(back(t, 1, 2))
                if active(s, 2):
                    invert(back(t, 2, 2), 0)
                if active(s, 0):
                    ln1(t)
                if active(s, 2):
                    invert(back(t, 2, 2), 1)
                if active(s, 1):
                    exp_ku(back(t, 1, 2))
                if active(s, 2):
                    start_y(back(t, 2, 2))
                if active(s, 0):
                    normalise(t)
                if active(s, 4):
                    ln2(back(t, 4, 2))
                if active(s, 3):
                    evacuate(back(t, 3, 2))

            act.wait_ge(const_in, 16)
            run(act, step, 0, LOOP1, STEPS, 2)
            nc.scalar.preload_act_table(ACT.Silu)

            def evacuate3(t):
                i, k = t
                wait(act, ngt_tr[k], i + 1)
                wait(act, gu_ready[k], i)
                nc.scalar.activation(ngt[k][:, :, :], ngt_ps[k % 2][:, 0:G * P].rearrange("p (g n) -> p g n", g=G),
                                     ACT.Copy).then_inc(ngt_ready[k], 1)

            def silu(t):
                i, k = t
                wait(act, gu_ready[k], i + 1)
                wait(act, hh_ready[k], i)
                nc.scalar.activation(sg[k][:, :], gu_ps[k % 2][:, 0:I], ACT.Silu).then_inc(sg_ready[k], 1)
                wait(act, xg_in[k], 16 * (i + 1))
                nc.scalar.activation(th[k][:, :], rows_of(t)[:, GAP:GAP + 1], ACT.Tanh, scale=0.5).then_inc(th_ready[k], 1)

            def step3(t, s):
                if live(s, 2):
                    evacuate3(ahead(t, 2))
                if live(s, 1):
                    silu(ahead(t, 1))

            evacuate3((0, 0))
            evacuate3((0, 1))
            silu((0, 0))
            run(act, step3, 0, LOOP3, TILES, 4)

        @blk.tensor
        def _(pe):
            pe.wait_ge(const_in, 16)
            pe.wait_ge(rwt_tr, 1)
            for g in range(G):
                last = nc.tensor.transpose(rwt_ps[:, g, :], rwc[:, g * P:(g + 1) * P], kc[0:E, K_ID:K_ID + E])
            last.then_inc(rwt_tr, 1)
            pe.wait_ge(rwt_ready, 1)
            pe.wait_ge(diag_ready, 1)

            def rows(t):
                i, h = t
                pi, ph = back(t, 1, 2)
                wait(pe, x2t_ready[h], 2 * i + 2)
                wait(pe, logit_read[ph], pi + 1)
                for q in range(2):
                    wait(pe, rows_read[ph], 2 * pi + q + 1)
                    for j in range(2):
                        cols = slice((2 * q + j) * P, (2 * q + j + 1) * P)
                        for g in range(G):
                            last = nc.tensor.transpose(rows_ps[q][:, j, g * P:(g + 1) * P], x2t[h][:, g, cols], ident)
                    last.then_inc(rows_ready[h], 1)
                    if q == 1:
                        continue
                    for j in range(JT):
                        for g in range(G):
                            last = nc.tensor.matmul(logit_ps[:, j, :], x2t[h][:, g, j * P:(j + 1) * P], rwt[:, g, :],
                                                    start=(g == 0), stop=(g == G - 1))
                    last.then_inc(logit_ready[h], 1)

            def read_out(t):
                i, h = t
                pi, ph = back(t, 1, 2)
                for g in range(G):
                    wait(pe, sv_ready[h], 2 * i + g + 1)
                    wait(pe, y_ready[ph], 2 * pi + g + 1)
                    nc.tensor.matmul(num_ps[g][:, :], diag[:, g, :], ev[h][:, g, :], start=True, stop=False)
                    nc.tensor.matmul(by_seq(num_ps[g][:, :])[:, :, 1:T], ident,
                                     by_seq(sv[h][:, g, :])[:, :, 0:T - 1],
                                     start=False, stop=True).then_inc(num_ready[h], 1)

            def to_channels(t):
                i, h = t
                pi, ph = back(t, 1, 2)
                wait(pe, xn_ready[h], i + 1)
                for g in range(G):
                    wait(pe, eb_ready[ph], 2 * pi + g + 1)
                    for j in range(JT):
                        last = nc.tensor.transpose(kt_ps[g][:, j * P:(j + 1) * P], xn[h][:, j, g * P:(g + 1) * P], ident)
                    last.then_inc(kt_ready[h], 1)

            def step(t, s):
                if active(s, 2):
                    read_out(back(t, 2, 2))
                if active(s, 3):
                    rows(back(t, 3, 2))
                if active(s, 0):
                    to_channels(t)

            run(pe, step, 0, LOOP1, STEPS, 2)

            pe.wait_ge(hot_ready, 1)
            nc.tensor.matmul(bank[0][:, 0:E * NT], lt_b[:, :], hot[:, :, :].rearrange("p e i -> p (e i)"), start=True, stop=True)
            nc.tensor.matmul(bank[1][:, 0:E * NT], one_b[:, :], hot[:, :, :].rearrange("p e i -> p (e i)"),
                             start=True, stop=True).then_inc(rank_ready, 1)
            pe.wait_ge(num_hi_ready, 1)
            for n in range(NT):
                if n % 8 == 0:
                    pe.wait_ge(at_lo_ready, n // 8 + 1)
                last = nc.tensor.matmul(id_ps, at_lo[:, n, :], num_hi[:, n, :, :].rearrange("p a t -> p (a t)"),
                                        start=(n == 0), stop=(n == NT - 1))
            last.then_inc(id_ready, 1)

            pe.wait_ge(table_ready, 1)
            pe.wait_ge(wgu_in, 16 * E)
            pe.wait_ge(wdn_in, 16 * E)

            def transpose_x(t):
                i, k = t
                bi, bk = back(t, 2, 4)
                wait(pe, ng_ready[k], i + 1)
                wait(pe, ngt_ready[bk], bi + 1)
                for g in range(G):
                    last = nc.tensor.transpose(ngt_ps[k % 2][:, g * P:(g + 1) * P], ng[k][:, g * P:(g + 1) * P], ident)
                last.then_inc(ngt_tr[k], 1)

            def round_experts(i):
                packed = nc.values_load(word[0:1, bass.ds(i, 1)], engines=[mybir.EngineType.PE], min_val=0,
                                        max_val=(1 << 5 * BITS) - 1,
                                        skip_runtime_bounds_check_because="five sums of E - 1 comparisons")
                return [(packed >> BITS * k) & (E - 1) for k in range(5)]

            def gate_up(t, e):
                i, k = t
                bi, bk = back(t, 2, 4)
                wait(pe, ngt_ready[k], i + 1)
                wait(pe, hh_ready[bk], bi + 1)
                for g in range(G):
                    last = nc.tensor.matmul(gu_ps[k % 2][:, 0:2 * I], ngt[k][:, g, :],
                                            wgu[:, g, bass.ds(e, 1), :].rearrange("p o n -> p (o n)"),
                                            start=(g == 0), stop=(g == G - 1))
                last.then_inc(gu_ready[k], 1)

            def transpose_h(t):
                i, k = t
                bi, bk = back(t, 2, 4)
                wait(pe, hh_ready[k], i + 1)
                wait(pe, hht_ready[bk], bi + 1)
                for a in range(2):
                    last = nc.tensor.transpose(hht_ps[k % 2][0:IH, a * P:(a + 1) * P], hh[k][:, a * IH:(a + 1) * IH], ident)
                last.then_inc(hht_tr[k], 1)

            def down(t, e):
                i, k = t
                bi, bk = back(t, 2, 4)
                wait(pe, hht_ready[k], i + 1)
                wait(pe, ob_ready[bk], bi + 1)
                for a in range(2):
                    last = nc.tensor.matmul(o_ps[k % 2][:, 0:C], hht[k][:, a, :],
                                            wdn[:, a, bass.ds(e, 1), :].rearrange("p o n -> p (o n)"),
                                            start=(a == 0), stop=(a == 1))
                last.then_inc(o_ready[k], 1)

            expert = []

            def step3(t, s):
                if t[1] == 0:
                    expert[:] = round_experts(t[0])
                if live(s, 2):
                    transpose_x(ahead(t, 2))
                transpose_h(t)
                if live(s, 1):
                    gate_up(ahead(t, 1), expert[t[1] + 1])
                down(t, expert[t[1]])

            transpose_x((0, 0))
            transpose_x((0, 1))
            gate_up((0, 0), round_experts(0)[0])
            run(pe, step3, 0, LOOP3, TILES, 4)

        @blk.vector
        def _(dve):
            vec = nc.vector
            dve.wait_ge(wu_in, 32)
            vec.tensor_scalar_min(bonus[:, :], wu[:, 1, :], U_MAX).then_inc(setup_v, 1)
            dve.wait_ge(setup_v, 1)
            vec.tensor_scalar(down_by[:, :], bonus[:, :], -1.0, 0.0, ALU.mult, ALU.min).then_inc(setup_v, 1)
            def setup():
                dve.wait_ge(rw_in, 16)
                vec.reduce_sum(rsum[:, :], rw[:, :], AX.X).then_inc(setup_v, 1)
                for g in range(G):
                    vec.memset(decay[g][:, :], 0.0)
                vec.memset(same_e[:, :, :], 1.0)
                vec.memset(one_b[:, :], 1.0)
                vec.memset(ones8[:, :], 1.0)
                vec.memset(expert_f[:, :], 0.0)
                vec.memset(row[0][:, :, GAP:ROW], 0.0)
                vec.memset(row[1][:, :, GAP:ROW], 0.0).then_inc(setup_v, 1)
                dve.wait_ge(setup_v, 4)
                vec.tensor_scalar_mul(rmean[:, :], rsum[:, :], 1.0 / C).then_inc(setup_v, 1)
                vec.memset(same_e[:, :, 0], 0.0)
                dve.wait_ge(setup_v, 5)
                vec.tensor_scalar_sub(rwc[:, :], rw[:, :], rmean[:, 0:1]).then_inc(rwt_tr, 1)
                dve.wait_ge(const_in, 16)
                vec.tensor_copy(lt_b[:, :], kc[:, K_LT:K_LT + P])
                vec.tensor_copy(iota_b[:, :], kc[:, K_IOTA:K_IOTA + P])
                dve.wait_ge(exp_wu_ready, 1)
                for g in range(G):
                    vec.tensor_copy(by_seq(decay[g][:, :])[:, :, 1:T],
                                    exp_w[:, g:g + 1].unsqueeze(2).to_broadcast([P, SEQ, T - 1]))
                    last = vec.tensor_scalar_mul(diag[:, g, :], ident, exp_u[:, g:g + 1])
                last.then_inc(diag_ready, 1)
                dve.wait_ge(diag_ready, 1)
                dve.wait_ge(rwt_tr, 2)
                vec.tensor_copy(rwt[:, :, :], rwt_ps).then_inc(rwt_ready, 1)

            def stats1(t):
                i, h = t
                wait(dve, x_in[h], 16 * (i + 1))
                wait(dve, xn_ready[h], i)
                for j in range(JT):
                    last = vec.bn_stats(six1[h][:, j, :], xr[h][:, j, :])
                last.then_inc(six1_ready[h], 1)
                wait_apart(dve, six1_ready[h], i + 1)
                for j in range(JT):
                    last = vec.bn_aggr(mv1[h][:, j, :], six1[h][:, j, :])
                last.then_inc(mv1_ready[h], 1)

            def shift1(t):
                i, h = t
                wait(dve, rstd1_ready[h], i + 1)
                vec.scalar_tensor_tensor(out=nmr1[h][:, :], in0=mv1[h][:, :, 0], scalar=-1.0, in1=rstd1[h][:, :],
                                         op0=ALU.mult, op1=ALU.mult).then_inc(nmr1_ready[h], 1)

            def scans(t):
                i, h = t
                wait(dve, num_ready[h], 2 * i)
                wait(dve, den_ready[h], 2 * i)
                for state, data, ready, done in ((sk, ek, ek_ready, sk_ready), (sv, ev, ev_ready, sv_ready)):
                    for g in range(G):
                        wait(dve, ready[h], 2 * i + g + 1)
                        vec.tensor_tensor_scan(state[h][:, g, :], decay[g][:, :], data[h][:, g, :], 0.0,
                                               ALU.mult, ALU.add).then_inc(done[h], 1)

            def divide(t):
                i, h = t
                wait(dve, x2t_ready[h], 2 * i)
                for g in range(G):
                    wait(dve, num_ready[h], 2 * i + g + 1)
                    wait(dve, rd_ready[h], 2 * i + g + 1)
                    vec.tensor_tensor(by_seq(yt[h][:, g, :])[:, :, 1:T], by_seq(num_ps[g][:, :])[:, :, 1:T],
                                      by_seq(eb[h][:, g, :])[:, :, 1:T], ALU.mult).then_inc(y_ready[h], 1)

            def stats2(t):
                i, h = t
                wait(dve, rows_out[h], 16 * i)
                wait(dve, logit_ready[h], i + 1)
                vec.tensor_copy(logit[:, bass.ds((2 * i + h) * JT, JT), :], logit_ps)
                for j in range(JT):
                    last = vec.max(top[h][:, j, :], logit_ps[:, j, :])
                last.then_inc(logit_read[h], 1)
                for j in range(JT):
                    if j % 2 == 0:
                        wait(dve, rows_read[h], 2 * i + j // 2 + 1)
                    last = vec.bn_stats(six2[h][:, j, :], row[h][:, j, 0:C])
                last.then_inc(six2_ready[h], 1)
                wait(dve, logit_read[h], i + 1)
                vec.tensor_sub(gap[h][:, :], top[h][:, :, 0], top[h][:, :, 1]).then_inc(gap_ready[h], 1)
                wait_apart(dve, six2_ready[h], i + 1)
                for j in range(JT):
                    last = vec.bn_aggr(row[h][:, j, MEAN:RSTD + 1], six2[h][:, j, :])
                last.then_inc(mv2_ready[h], 1)

            def scale_gap(t):
                i, h = t
                wait(dve, rstd2_ready[h], i + 1)
                wait(dve, gap_ready[h], i + 1)
                vec.tensor_tensor(row[h][:, :, GAP], gap[h][:, :], row[h][:, :, RSTD], ALU.mult)\
                    .then_inc(row_ready[h], 1)

            def step(t, s):
                if active(s, 0):
                    stats1(t)
                if active(s, 4):
                    stats2(back(t, 4, 2))
                if active(s, 0):
                    shift1(t)
                if active(s, 2):
                    divide(back(t, 2, 2))
                if active(s, 1):
                    scans(back(t, 1, 2))
                if active(s, 4):
                    scale_gap(back(t, 4, 2))

            stats1((0, 0))
            shift1((0, 0))
            setup()
            run(dve, step, 1, LOOP1, STEPS, 2)

            done = [0]

            def link(ins):
                done[0] += 1
                ins.then_inc(route_v, 1)
                dve.wait_ge(route_v, done[0])

            wide = [P, NT, E]
            for h in range(2):
                dve.wait_ge(row_ready[h], BLOCKS // 2)
            link(vec.tensor_reduce(best[:, :], logit[:, :, :], AX.X, ALU.max))
            link(vec.tensor_tensor(is_best[:, :, :], logit[:, :, :], best[:, :].unsqueeze(2).to_broadcast(wide), ALU.is_ge))
            e8 = kc[:, K_E8:K_E8 + E].unsqueeze(1).to_broadcast(wide)
            link(vec.tensor_tensor(cand[:, :, :], is_best[:, :, :], e8, ALU.mult))
            link(vec.tensor_reduce(first[:, :], cand[:, :, :], AX.X, ALU.min))
            vec.tensor_tensor(hot[:, :, :].rearrange("p e i -> p i e"), e8,
                              first[:, :].unsqueeze(2).to_broadcast(wide), ALU.is_equal).then_inc(hot_ready, 1)
            dve.wait_ge(rank_ready, 1)
            dve.wait_ge(hot_ready, 1)
            link(vec.tensor_tensor_scan(upto[:, :, :].rearrange("p e i -> p (e i)"), same_e[:, :, :].rearrange("p e i -> p (e i)"),
                                        bank[1][:, 0:E * NT], 0.0, ALU.mult, ALU.add))
            link(vec.tensor_scalar_add(cnt_i[:, :], upto[:, :, NT - 1], float(P - 1)))
            link(vec.tensor_single_scalar(nt_i[:, :], cnt_i[:, :], 7, ALU.arith_shift_right))
            link(vec.tensor_copy(nt_f[:, :], nt_i[:, :]))
            link(vec.tensor_tensor_scan(end_f[:, :], ones8[:, :], nt_f[:, :], 0.0, ALU.mult, ALU.add))
            vec.tensor_tensor(before[:, :, :], upto[:, :, :], tot_ps, ALU.subtract)
            link(vec.tensor_sub(base[:, :], end_f[:, :], nt_f[:, :]))
            link(vec.tensor_tensor(slot3[:, :, :], before[:, :, :], rank_ps, ALU.add))
            link(vec.scalar_tensor_tensor(out=before[:, :, :], in0=base[:, :].unsqueeze(2).to_broadcast([P, E, NT]),
                                          scalar=float(P), in1=slot3[:, :, :], op0=ALU.mult, op1=ALU.add))
            link(vec.tensor_tensor(slot3[:, :, :], before[:, :, :], hot[:, :, :], ALU.mult))
            link(vec.reduce_sum(slot[:, :], slot3[:, :, :].rearrange("p e i -> p i e"), AX.X))
            link(vec.tensor_copy(slot_i[:, :], slot[:, :]))
            vec.tensor_single_scalar(lo_i[:, :], slot_i[:, :], P - 1, ALU.bitwise_and)
            link(vec.tensor_single_scalar(hi_i[:, :], slot_i[:, :], 7, ALU.arith_shift_right))
            vec.tensor_copy(lo_f[:, :], lo_i[:, :])
            link(vec.tensor_copy(hi_f[:, :], hi_i[:, :]))
            per_tile = [P, NT, TILES]
            link(vec.tensor_tensor(at_hi[:, :, :], kc[:, K_IOTA:K_IOTA + TILES].unsqueeze(1).to_broadcast(per_tile),
                                   hi_f[:, :].unsqueeze(2).to_broadcast(per_tile), ALU.is_equal))
            vec.tensor_tensor(num_hi[:, :, 0, :], at_hi[:, :, :],
                              kc[:, K_TILE:K_TILE + NT].unsqueeze(2).to_broadcast(per_tile), ALU.mult)
            vec.tensor_scalar_mul(num_hi[:, :, 1, :], at_hi[:, :, :], kc[:, K_P:K_P + 1]).then_inc(num_hi_ready, 1)
            for n in range(NT):
                last = vec.tensor_scalar(at_lo[:, n, :], iota_b[:, :], lo_f[:, n:n + 1], None, ALU.is_equal)
                if n % 8 == 7:
                    last.then_inc(at_lo_ready, 1)
            shape = [1, TILES, E]
            link(vec.tensor_tensor(past[:, :, :], kc[0:1, K_IOTA:K_IOTA + TILES].unsqueeze(2).to_broadcast(shape),
                                   end_f[0:1, :].unsqueeze(1).to_broadcast(shape), ALU.is_ge))
            link(vec.reduce_sum(expert_f[:, 0:TILES], past[:, :, 0:E - 1], AX.X))
            link(vec.tensor_tensor(shifted[:, :, :], expert_f[:, 0:4 * ROUNDS].rearrange("p (r k) -> p r k", k=4),
                                   kc[0:1, K_POW:K_POW + 4].unsqueeze(1).to_broadcast([1, ROUNDS, 4]), ALU.mult))
            link(vec.reduce_sum(word_f[:, :], shifted[:, :, :], AX.X))
            link(vec.scalar_tensor_tensor(out=word[:, :], in0=expert_f[:, 4:4 * ROUNDS + 4:4], scalar=float(1 << 4 * BITS),
                                          in1=word_f[:, :], op0=ALU.mult, op1=ALU.add))
            dve.wait_ge(id_ready, 1)
            link(vec.tensor_scalar(id_hi[:, :], id_ps[:, 0:TILES], float(P), float(PAD_ID), ALU.mult, ALU.add))
            link(vec.tensor_tensor(id_f[:, :], id_hi[:, :], id_ps[:, TILES:2 * TILES], ALU.add))
            link(vec.tensor_copy(put_id[:, :], id_f[:, :]))
            vec.tensor_single_scalar(get_id[:, :], put_id[:, :], TOK - 1, ALU.bitwise_and).then_inc(table_ready, 1)

            def normalise3(t):
                i, k = t
                wait(dve, xg_in[k], 16 * (i + 1))
                wait(dve, ngt_tr[k], i)
                xt_ = rows_of(t)
                vec.tensor_scalar(ng[k][:, :], xt_[:, 0:C], xt_[:, MEAN:MEAN + 1], xt_[:, RSTD:RSTD + 1],
                                  ALU.subtract, ALU.mult).then_inc(ng_ready[k], 1)

            def hidden(t):
                i, k = t
                wait(dve, sg_ready[k], i + 1)
                wait(dve, hht_tr[k], i)
                vec.tensor_tensor(hh[k][:, :], gu_ps[k % 2][:, I:2 * I], sg[k][:, :], ALU.mult).then_inc(hh_ready[k], 1)
                wait(dve, th_ready[k], i + 1)
                vec.tensor_scalar(wt[k][:, :], th[k][:, :], 0.5, 0.5, ALU.mult, ALU.add).then_inc(wt_ready[k], 1)

            def evacuate_h(t):
                i, k = t
                wait(dve, hht_tr[k], i + 1)
                wait(dve, o_ready[k], i)
                vec.tensor_copy(hht[k][:, :, :], hht_ps[k % 2][0:IH, 0:2 * P].rearrange("p (a n) -> p a n", a=2))\
                    .then_inc(hht_ready[k], 1)

            def finish(t):
                i, k = t
                wait(dve, o_ready[k], i + 1)
                wait(dve, wt_ready[k], i + 1)
                wait(dve, put_out[k], 16 * i)
                vec.scalar_tensor_tensor(out=ob[k][:, :], in0=o_ps[k % 2][:, 0:C], scalar=wt[k][:, 0:1],
                                         in1=rows_of(t)[:, 0:C], op0=ALU.mult, op1=ALU.add).then_inc(ob_ready[k], 1)

            def step3(t, s):
                if live(s, 3):
                    normalise3(ahead(t, 3))
                evacuate_h(t)
                if live(s, 1):
                    hidden(ahead(t, 1))
                finish(t)

            for s in range(3):
                normalise3((0, s))
            hidden((0, 0))
            run(dve, step3, 0, LOOP3, TILES, 4)


def kernel(x, ctx_2048, L0_xattn_w, L0_xattn_u, L0_ffn_router_w, L0_ffn_gate_w, L0_ffn_up_w, L0_ffn_down_w):
    import concourse.bacc as bacc
    from concourse.bass_utils import run_bass_kernel_spmd

    def dense(a):
        return np.ascontiguousarray(a)

    x, c = np.asarray(x).reshape(TOK, C), np.asarray(ctx_2048).reshape(TOK, C)
    gate_up = np.concatenate([np.asarray(L0_ffn_gate_w), np.asarray(L0_ffn_up_w)], axis=1)
    arrays = {
        "x": dense(x),
        "x_t": dense(x.T),
        "ctx_t": dense(c.T),
        "w": dense(np.asarray(L0_xattn_w).reshape(G, P).T),
        "u": dense(np.asarray(L0_xattn_u).reshape(G, P).T),
        "router": dense(L0_ffn_router_w),
        "gate_up_t": dense(gate_up.transpose(2, 0, 1)),
        "down_t": dense(np.asarray(L0_ffn_down_w).transpose(2, 0, 1)),
        "consts": constants(),
    }
    nc = bacc.Bacc("TRN2", target_bir_lowering=False, num_devices=1)
    args = [nc.dram_tensor(n, a.shape, mybir.dt.from_np(a.dtype), kind="ExternalInput").ap() for n, a in arrays.items()]
    out = nc.dram_tensor("out", (TOK, C), F32, kind="ExternalOutput").ap()
    build(nc, *args, out)
    r = run_bass_kernel_spmd(nc, [arrays], core_ids=[0])
    return r.results[0]["out"].reshape(B, T, C)
```

```python
from contextlib import ExitStack

import numpy as np
import concourse.bass as bass
from concourse import mybir

P = 128
B, T, C = 64, 64, 256
TOK = B * T
G = C // P
NB = 512
BLOCKS = TOK // NB
JT = NB // P
SEQ = NB // T
NT = TOK // P
E, I = 8, 176
IH = I // 2
BITS = 3
TILES = (TOK + E * (P - 1)) // P
ROUNDS = (TILES + 3) // 4
ROW = C + 4
MEAN, RSTD, GAP = C, C + 1, C + 2
PAD_ID = 2 * TOK
EPS = 1e-5
HALF = (P - 1) / 2
ROUNDER = float(3 << 22)
U_MAX = 56.0

F32, BF16, I32 = mybir.dt.float32, mybir.dt.bfloat16, mybir.dt.int32
ALU = mybir.AluOpType
ACT = mybir.ActivationFunctionType
AX = mybir.AxisListType

K_ID, K_ORDER, K_IOTA, K_E8, K_TILE, K_P, K_EPS, K_ONE, K_POW = 0, 128, 256, 384, 392, 424, 425, 426, 427
K_ALL = 431


def constants():
    k = np.zeros((P, K_ALL), np.float32)
    p = np.arange(P)
    k[:, K_ID:K_ID + P] = np.eye(P)
    k[:, K_ORDER:K_ORDER + P] = (p[:, None] < p[None, :]) - 1.0
    k[:, K_IOTA:K_IOTA + P] = p[None, :]
    k[:, K_E8:K_E8 + E] = np.arange(E) - E
    k[:, K_TILE:K_TILE + NT] = np.arange(NT) - PAD_ID // P
    k[:, K_P] = p
    k[:, K_EPS] = EPS
    k[:, K_ONE] = 1.0
    k[:, K_POW:K_POW + 4] = 8.0 ** np.arange(4)
    return k


def build(nc, x, x_t, ctx_t, w, u, router, gate_up_t, down_t, consts, out):
    ctx = ExitStack()
    with ctx:
        def sb(name, shape, dt=F32):
            return ctx.enter_context(nc.sbuf_tensor(name, shape, dt))

        def sem(name):
            return ctx.enter_context(nc.semaphore(name))

        def sems(name, n):
            return [sem(f"{name}{k}") for k in range(n)]

        def wait(eng, s, value):
            if not (isinstance(value, int) and value <= 0):
                eng.wait_ge(s, value)

        scratch = nc.dram_tensor("x2_rows", (TOK, ROW), F32, kind="Internal").ap()

        kc = sb("kc", [P, K_ALL])
        ident = kc[:, K_ID:K_ID + P]
        wgu = sb("wgu", [P, G, E, 2 * I])
        wdn = sb("wdn", [IH, 2, E, C])
        wu = sb("wu", [P, 2, G])
        bonus = sb("bonus", [P, G])
        down_by = sb("down_by", [P, G])
        exp_w = sb("exp_w", [P, G])
        exp_u = sb("exp_u", [P, G])
        shrink = sb("shrink", [P, G])
        diag = sb("diag", [P, G, P])
        rw = sb("rw", [E, C])
        rsum = sb("rsum", [E, 1])
        rmean = sb("rmean", [E, 1])
        rwc = sb("rwc", [E, C])
        rwt = sb("rwt", [P, G, E])

        def two(name, shape, dt=F32):
            return [sb(f"{name}{h}", shape, dt) for h in range(2)]

        pool_w = JT * C
        assert TILES * ROW <= 10 * pool_w and G * NB == pool_w
        shared = sb("shared", [P, 10 * pool_w])
        xg = shared[:, 0:TILES * ROW].rearrange("p (n c) -> p n c", c=ROW)

        def pair(n, inner):
            return [shared[:, k * pool_w:(k + 1) * pool_w].rearrange("p (a b) -> p a b", b=inner)
                    for k in (2 * n, 2 * n + 1)]

        xr = pair(0, C)
        xn = pair(1, C)
        xt = pair(2, NB)
        vt = pair(3, NB)
        ek = pair(4, NB)
        eb = two("eb", [P, G, NB])
        ev = two("ev", [P, G, NB])
        sk = two("sk", [P, G, NB])
        sv = two("sv", [P, G, NB])
        decay = two("decay", [P, NB])
        yt = two("yt", [P, G, NB])
        x2t = two("x2t", [P, G, NB])
        row = two("row", [P, JT, ROW])
        six1 = two("six1", [P, JT, 6])
        mv1 = two("mv1", [P, JT, 2])
        lnv1 = two("lnv1", [P, JT])
        rstd1 = two("rstd1", [P, JT])
        nmr1 = two("nmr1", [P, JT])
        six2 = two("six2", [P, JT, 6])
        lnv2 = two("lnv2", [P, JT])
        top = two("top", [P, JT, 8])
        gap = two("gap", [P, JT])
        logit = sb("logit", [P, NT, E])

        best = sb("best", [P, NT])
        is_best = sb("is_best", [P, NT, E])
        cand = sb("cand", [P, NT, E])
        first = sb("first", [P, NT])
        hot = sb("hot", [P, E, NT], BF16)
        order_b = sb("order_b", [P, P], BF16)
        one_b = sb("one_b", [P, P], BF16)
        iota_b = sb("iota_b", [P, P], BF16)
        tile_b = sb("tile_b", [P, NT], BF16)
        same_e = sb("same_e", [P, E, NT])
        ones8 = sb("ones8", [P, E])
        upto = sb("upto", [P, E, NT])
        based = sb("based", [P, E, NT])
        slot3 = sb("slot3", [P, E, NT])
        part_nt = sb("part_nt", [P, E])
        nt_f = sb("nt_f", [P, E])
        end_f = sb("end_f", [P, E])
        base = sb("base", [P, E])
        slot = sb("slot", [P, NT])
        part_hi = sb("part_hi", [P, NT])
        lo_b = sb("lo_b", [P, NT], BF16)
        hi_b = sb("hi_b", [P, NT], BF16)
        at_lo = sb("at_lo", [P, NT, P], BF16)
        at_hi = sb("at_hi", [P, NT, TILES], BF16)
        num_hi = sb("num_hi", [P, NT, 2, TILES], BF16)
        id_hi = sb("id_hi", [P, TILES])
        id_f = sb("id_f", [P, TILES])
        put_id = sb("put_id", [P, TILES], I32)
        get_id = sb("get_id", [P, TILES], I32)
        past = sb("past", [1, TILES, E])
        expert_f = sb("expert_f", [1, 4 * ROUNDS + 4])
        shifted = sb("shifted", [1, ROUNDS, 4])
        word_f = sb("word_f", [1, ROUNDS])
        word = sb("word", [1, ROUNDS], I32)

        def four(name, shape, dt=F32):
            return [sb(f"{name}{k}", shape, dt) for k in range(4)]

        ng = four("ng", [P, C])
        ngt = four("ngt", [P, G, P])
        sg = four("sg", [P, I])
        hh = four("hh", [P, I])
        hht = four("hht", [IH, 2, P])
        th = four("th", [P, 1])
        wt = four("wt", [P, 1])
        ob = four("ob", [P, C])

        bank = [ctx.enter_context(nc.psum_tensor(f"bank{n}", [P, 512], F32)) for n in range(8)]
        kt_ps, num_ps = bank[0:2], bank[4:6]
        rows_ps = [bank[n][:, :].rearrange("p (j c) -> p j c", j=2) for n in (2, 6)]
        logit_ps = bank[7][:, 0:JT * E].rearrange("p (j e) -> p j e", e=E)
        rwt_ps = bank[7][:, 0:G * E].rearrange("p (g e) -> p g e", e=E)
        rank_ps = bank[0][:, 0:E * NT].rearrange("p (e i) -> p e i", e=E)
        tot_ps = bank[1][:, 0:E * NT]
        id_ps = bank[2][:, 0:2 * TILES]
        ngt_ps, gu_ps, hht_ps, o_ps = bank[0:2], bank[2:4], bank[4:6], bank[6:8]

        const_in, wu_in, rw_in, wgu_in, wdn_in = (sem(n) for n in (
            "const_in", "wu_in", "rw_in", "wgu_in", "wdn_in"))
        fills_ready, decay_ready = (sem(n) for n in ("fills_ready", "decay_ready"))
        setup_v, exp_wu_ready, diag_ready, rwt_tr, rwt_ready = (sem(n) for n in (
            "setup_v", "exp_wu_ready", "diag_ready", "rwt_tr", "rwt_ready"))
        x_in, xt_in, v_in, rows_out = (sems(n, 2) for n in ("x_in", "xt_in", "v_in", "rows_out"))
        six1_ready, mv1_ready, lnv1_ready, rstd1_ready, nmr1_ready, xn_ready = (sems(n, 2) for n in (
            "six1_ready", "mv1_ready", "lnv1_ready", "rstd1_ready", "nmr1_ready", "xn_ready"))
        kt_ready, ek_ready, eb_ready, ev_ready, sv_ready, sk_ready = (sems(n, 2) for n in (
            "kt_ready", "ek_ready", "eb_ready", "ev_ready", "sv_ready", "sk_ready"))
        den_ready, num_ready, lnd_ready, rd_ready, y0_ready, y_ready, x2t_ready = (sems(n, 2) for n in (
            "den_ready", "num_ready", "lnd_ready", "rd_ready", "y0_ready", "y_ready", "x2t_ready"))
        rows_ready, rows_read, logit_ready, logit_read = (sems(n, 2) for n in (
            "rows_ready", "rows_read", "logit_ready", "logit_read"))
        six2_ready, mv2_ready, lnv2_ready, rstd2_ready, gap_ready, row_ready = (sems(n, 2) for n in (
            "six2_ready", "mv2_ready", "lnv2_ready", "rstd2_ready", "gap_ready", "row_ready"))
        route_v, hot_ready, rank_ready, lo_ready, at_hi_ready, num_hi_ready = (sem(n) for n in (
            "route_v", "hot_ready", "rank_ready", "lo_ready", "at_hi_ready", "num_hi_ready"))
        off_lo_ready, off_sq_ready, at_lo_dve, at_lo_act, id_ready, table_ready, word_ready = (sem(n) for n in (
            "off_lo_ready", "off_sq_ready", "at_lo_dve", "at_lo_act", "id_ready", "table_ready", "word_ready"))
        xg_in, ng_ready, ngt_tr, ngt_ready, gu_ready, sg_ready, hh_ready = (sems(n, 4) for n in (
            "xg_in", "ng_ready", "ngt_tr", "ngt_ready", "gu_ready", "sg_ready", "hh_ready"))
        hht_tr, hht_ready, th_ready, wt_ready, o_ready, ob_ready, put_out = (sems(n, 4) for n in (
            "hht_tr", "hht_ready", "th_ready", "wt_ready", "o_ready", "ob_ready", "put_out"))

        def wait_apart(eng, s, value):
            eng.wait_ge(const_in, 16)
            wait(eng, s, value)

        def back(t, n, slots):
            i, k = t
            k -= n
            while k < 0:
                k += slots
                i = i - 1
            return i, k

        def rows_of(t):
            i, k = t
            return xg[:, bass.ds(4 * i + k, 1), :].rearrange("p o c -> p (o c)")

        def ahead2(t):
            i, h = t
            return (i, 1) if h == 0 else (i + 1, 0)

        def ahead(t, n):
            i, k = t
            return (i, k + n) if k + n < 4 else (i + 1, k + n - 4)

        def run_blocks(step, first, last):
            for s in range(first, last):
                step((s // 2, s % 2), s)

        def run_tiles(eng, step):
            whole = TILES // 4
            assert whole % 2 == 1
            for s in range(4):
                step((0, s), s)
            with eng.Fori(0, (whole - 1) // 2) as two_rounds:
                for i in (two_rounds * 2 + 1, two_rounds * 2 + 2):
                    for k in range(4):
                        step((i, k), None)
            for s in range(4 * whole, TILES):
                step((s // 4, s % 4), s)

        LO_DVE, LO_ACT = ((0, 7), (7, 14), (14, 21)), ((21, 27), (27, 32))

        def lo_args(a, b):
            part = [P, b - a, P]
            return (at_lo[:, a:b, :], iota_b[:, :].unsqueeze(1).to_broadcast(part),
                    lo_b[:, a:b].unsqueeze(2).to_broadcast(part))

        LAG = 4
        STEPS = BLOCKS + LAG

        def active(s, lag):
            return 0 <= s - lag < BLOCKS

        def live(s, n):
            return s is None or s + n < TILES

        x_v = x.rearrange("(b j p) c -> p b j c", j=JT, p=P)
        xt_v = x_t.rearrange("(g p) (b n) -> p b g n", p=P, n=NB)
        ct_v = ctx_t.rearrange("(g p) (b n) -> p b g n", p=P, n=NB)
        sc_v = scratch.rearrange("(b j p) c -> p b j c", j=JT, p=P)

        def by_seq(a):
            return a.rearrange("p (s t) -> p s t", t=T)

        blk = ctx.enter_context(nc.Block())

        @blk.sync
        def _(sp):
            def load_rows(t):
                i, h = t
                wait(sp, xn_ready[h], 2 * i)
                sp.dma_start(xr[h][:, :, :], x_v[:, 2 * i + h]).then_inc(x_in[h], 16)

            def load_ctx(t):
                i, h = t
                wait(sp, ev_ready[h], 2 * i)
                wait(sp, y0_ready[h], i)
                sp.dma_start(vt[h][:, :, :], ct_v[:, 2 * i + h]).then_inc(v_in[h], 16)

            def load_columns(t):
                i, h = t
                wait(sp, x2t_ready[h], 2 * i)
                sp.dma_start(xt[h][:, :, :], xt_v[:, 2 * i + h]).then_inc(xt_in[h], 16)

            def load_expert(e):
                sp.dma_start(wgu[:, :, e, :], gate_up_t[:, e, :].rearrange("(g p) n -> p g n", p=P)).then_inc(wgu_in, 16)
                sp.dma_start(wdn[:, :, e, :], down_t[:, e, :].rearrange("(a p) n -> p a n", p=IH)).then_inc(wdn_in, 16)

            def store(t):
                i, h = t
                wait(sp, row_ready[h], i + 1)
                sp.dma_start(sc_v[:, 2 * i + h], row[h][:, :, :]).then_inc(rows_out[h], 16)

            def step(t, s):
                if active(s, -1):
                    load_rows(ahead2(t))
                if active(s, 1):
                    load_columns(back(t, 1, 2))
                if active(s, 0):
                    load_ctx(t)
                if active(s, 2):
                    load_expert(s - 2)
                if active(s, LAG):
                    store(back(t, LAG, 2))

            load_rows((0, 0))
            run_blocks(step, 0, STEPS)
            for k in range(4):
                wait(sp, put_out[k], 16 * len(range(k, TILES, 4)))

        @blk.gpsimd
        def _(pool):
            def weigh(t):
                i, h = t
                wait(pool, v_in[h], 16 * (i + 1))
                wait(pool, num_ready[h], 2 * i)
                for g in range(G):
                    wait(pool, ek_ready[h], 2 * i + g + 1)
                    nc.gpsimd.tensor_tensor(ev[h][:, g, :], ek[h][:, g, :], vt[h][:, g, :],
                                            ALU.mult).then_inc(ev_ready[h], 1)

            def residual(t):
                i, h = t
                wait(pool, xt_in[h], 16 * (i + 1))
                wait(pool, y0_ready[h], i + 1)
                wait(pool, rows_ready[h], 2 * i)
                wait(pool, logit_ready[h], i)
                for g in range(G if 2 * i + h < BLOCKS - 1 else 1):
                    wait(pool, y_ready[h], 2 * i + g + 1)
                    nc.gpsimd.tensor_tensor(x2t[h][:, g, :], yt[h][:, g, :], xt[h][:, g, :],
                                            ALU.add).then_inc(x2t_ready[h], 1)

            def denominator(t):
                i, h = t
                for g in range(G):
                    wait(pool, eb_ready[h], 2 * i + g + 1)
                    wait(pool, sk_ready[h], 2 * i + g + 1)
                    now = by_seq(eb[h][:, g, :])[:, :, 1:T]
                    nc.gpsimd.tensor_tensor(now, now, by_seq(sk[h][:, g, :])[:, :, 0:T - 1], ALU.add)\
                        .then_inc(den_ready[h], 1)

            def normalise_last(t):
                i, h = t
                wait(pool, x_in[h], 16 * (i + 1))
                wait(pool, nmr1_ready[h], i + 1)
                wait(pool, kt_ready[h], 2 * i)
                j = JT - 1
                nc.gpsimd.tensor_scalar(xn[h][:, j, :], xr[h][:, j, :], rstd1[h][:, j:j + 1], nmr1[h][:, j:j + 1],
                                        ALU.mult, ALU.add).then_inc(xn_ready[h], 1)

            def step(t, s):
                if active(s, 2):
                    denominator(back(t, 2, 2))
                if active(s, 1):
                    weigh(back(t, 1, 2))
                if active(s, 0):
                    normalise_last(t)
                if active(s, 2):
                    residual(back(t, 2, 2))

            nc.gpsimd.memset(same_e[:, :, 1:NT], 1.0)
            nc.gpsimd.memset(same_e[:, :, 0:1], 0.0)
            for g in range(G):
                nc.gpsimd.memset(decay[g][:, :], 0.0)
            nc.gpsimd.memset(one_b[:, :], 1.0)
            nc.gpsimd.memset(ones8[:, :], 1.0)
            nc.gpsimd.memset(expert_f[:, :], 0.0)
            nc.gpsimd.memset(row[0][:, :, GAP:ROW], 0.0)
            nc.gpsimd.memset(row[1][:, :, GAP:ROW], 0.0).then_inc(fills_ready, 1)
            run_blocks(step, 0, STEPS)

            pool.wait_ge(lo_ready, 1)
            for a, b in LO_ACT:
                nc.gpsimd.tensor_tensor(*lo_args(a, b), ALU.subtract).then_inc(off_lo_ready, 1)

            for h in range(2):
                wait(pool, rows_out[h], 16 * (BLOCKS // 2))
            pool.wait_ge(table_ready, 1)

            def gather(n):
                wait(pool, ng_ready[n % 4], n // 4)
                pool.indirect_dma_start(
                    out=xg[:, n, :], out_offset=None, in_=scratch,
                    in_offset=bass.IndirectOffsetOnAxis(ap=get_id[:, n:n + 1], axis=0)).then_inc(xg_in[n % 4], 16)

            def scatter(n):
                wait(pool, ob_ready[n % 4], n // 4 + 1)
                pool.indirect_dma_start(
                    out=out, out_offset=bass.IndirectOffsetOnAxis(ap=put_id[:, n:n + 1], axis=0),
                    in_=ob[n % 4][:, :], in_offset=None, bounds_check=TOK - 1, oob_is_err=False)\
                    .then_inc(put_out[n % 4], 16)

            LEAD = 7
            for n in range(LEAD):
                gather(n)
            for n in range(TILES):
                if n + LEAD < TILES:
                    gather(n + LEAD)
                scatter(n)

        @blk.scalar
        def _(act):
            act.dma_start(kc[:, :], consts).then_inc(const_in, 16)
            act.dma_start(wu[:, 0, :], w).then_inc(wu_in, 16)
            act.dma_start(wu[:, 1, :], u).then_inc(wu_in, 16)
            act.dma_start(rw[:, :], router).then_inc(rw_in, 16)
            nc.scalar.preload_act_table_set("natural_log_exp_and_others")

            def evacuate(t, q):
                i, h = t
                wait(act, rows_out[h], 16 * i)
                wait(act, rows_ready[h], 2 * i + q + 1)
                nc.scalar.activation(row[h][:, 2 * q:2 * q + 2, 0:C], rows_ps[q], ACT.Copy).then_inc(rows_read[h], 1)

            def ln2(t):
                i, h = t
                wait(act, mv2_ready[h], i + 1)
                nc.scalar.activation(lnv2[h][:, :], row[h][:, :, RSTD], ACT.Ln, bias=kc[:, K_EPS:K_EPS + 1])\
                    .then_inc(lnv2_ready[h], 1)

            def rstd2(t):
                i, h = t
                wait(act, lnv2_ready[h], i + 1)
                nc.scalar.activation(row[h][:, :, RSTD], lnv2[h][:, :], ACT.Exp, scale=-0.5).then_inc(rstd2_ready[h], 1)

            def exp_k(t, g):
                i, h = t
                wait(act, ev_ready[h], 2 * i)
                wait(act, sk_ready[h], 2 * i)
                wait(act, kt_ready[h], 2 * i + g + 1)
                nc.scalar.activation(ek[h][:, g, :], kt_ps[g][:, :], ACT.Exp).then_inc(ek_ready[h], 1)

            def exp_ku(t, g):
                i, h = t
                wait(act, y_ready[h], 2 * i)
                nc.scalar.activation(eb[h][:, g, :], kt_ps[g][:, :], ACT.Exp, bias=bonus[:, g:g + 1])\
                    .then_inc(eb_ready[h], 1)

            def log_den(t, g):
                i, h = t
                wait(act, den_ready[h], 2 * i + g + 1)
                now = by_seq(eb[h][:, g, :])[:, :, 1:T]
                nc.scalar.activation(now, now, ACT.Ln, scale=shrink[:, g:g + 1]).then_inc(lnd_ready[h], 1)

            def invert(t, g):
                i, h = t
                wait(act, lnd_ready[h], 2 * i + g + 1)
                now = by_seq(eb[h][:, g, :])[:, :, 1:T]
                nc.scalar.activation(now, now, ACT.Exp, bias=down_by[:, g:g + 1], scale=-1.0).then_inc(rd_ready[h], 1)

            def start_y(t):
                i, h = t
                wait(act, v_in[h], 16 * (i + 1))
                wait(act, x2t_ready[h], 2 * i)
                nc.scalar.activation(yt[h][:, :, 0:NB:T], vt[h][:, :, 0:NB:T], ACT.Copy).then_inc(y0_ready[h], 1)

            def exp_wu():
                act.wait_ge(wu_in, 32)
                act.wait_ge(setup_v, 2)
                nc.scalar.activation(exp_w[:, :], wu[:, 0, :], ACT.Exp)
                nc.scalar.activation(shrink[:, :], down_by[:, :], ACT.Exp)
                nc.scalar.activation(exp_u[:, :], bonus[:, :], ACT.Exp).then_inc(exp_wu_ready, 1)

            def ln1(t):
                i, h = t
                wait(act, mv1_ready[h], i + 1)
                nc.scalar.activation(lnv1[h][:, :], mv1[h][:, :, 1], ACT.Ln, bias=kc[:, K_EPS:K_EPS + 1])\
                    .then_inc(lnv1_ready[h], 1)

            def get_rstd1(t):
                i, h = t
                wait(act, lnv1_ready[h], i + 1)
                nc.scalar.activation(rstd1[h][:, :], lnv1[h][:, :], ACT.Exp, scale=-0.5).then_inc(rstd1_ready[h], 1)

            def normalise(t):
                i, h = t
                wait(act, x_in[h], 16 * (i + 1))
                wait(act, nmr1_ready[h], i + 1)
                wait(act, kt_ready[h], 2 * i)
                for j in range(JT - 1):
                    last = nc.scalar.activation(xn[h][:, j, :], xr[h][:, j, :], ACT.Identity,
                                                bias=nmr1[h][:, j:j + 1], scale=rstd1[h][:, j:j + 1])
                last.then_inc(xn_ready[h], 1)

            def step(t, s):
                before, before2, before3, before4 = (back(t, n, 2) for n in range(1, 5))
                if active(s, 2):
                    start_y(before2)
                if active(s, 1):
                    exp_k(before, 0)
                if active(s, 1):
                    exp_k(before, 1)
                if active(s, 2):
                    log_den(before2, 0)
                if active(s, 0):
                    ln1(t)
                if active(s, 2):
                    invert(before2, 0)
                if active(s, 0):
                    get_rstd1(t)
                if active(s, 2):
                    log_den(before2, 1)
                if active(s, 1):
                    exp_ku(before, 0)
                if active(s, 2):
                    invert(before2, 1)
                if active(s, 1):
                    exp_ku(before, 1)
                if active(s, 0):
                    normalise(t)
                early = s < STEPS - 2
                if active(s, 4) and early:
                    ln2(before4)
                if active(s, 3):
                    evacuate(before3, 0)
                if active(s, 4) and early:
                    rstd2(before4)
                if active(s, 3):
                    evacuate(before3, 1)
                if not early:
                    ln2(before4)
                    rstd2(before4)

            act.wait_ge(const_in, 16)
            ln1((0, 0))
            get_rstd1((0, 0))
            normalise((0, 0))
            exp_wu()
            run_blocks(step, 1, STEPS)
            nc.scalar.preload_act_table(ACT.Silu)

            act.wait_ge(at_hi_ready, 1)
            nc.scalar.activation(num_hi[:, :, 1, :], at_hi[:, :, :], ACT.Copy, scale=kc[:, K_P:K_P + 1])\
                .then_inc(num_hi_ready, 1)
            for c, (a, b) in enumerate(LO_ACT):
                act.wait_ge(off_lo_ready, c + 1)
                nc.scalar.activation(at_lo[:, a:b, :], at_lo[:, a:b, :], ACT.Square).then_inc(off_sq_ready, 1)
                act.wait_ge(off_sq_ready, c + 1)
                nc.scalar.activation(at_lo[:, a:b, :], at_lo[:, a:b, :], ACT.Relu, bias=kc[:, K_ONE:K_ONE + 1], scale=-1.0)\
                    .then_inc(at_lo_act, 1)

            def evacuate3(t):
                i, k = t
                wait(act, ngt_tr[k], i + 1)
                wait(act, gu_ready[k], i)
                nc.scalar.activation(ngt[k][:, :, :], ngt_ps[k % 2][:, 0:G * P].rearrange("p (g n) -> p g n", g=G),
                                     ACT.Copy).then_inc(ngt_ready[k], 1)

            def silu(t):
                i, k = t
                wait(act, gu_ready[k], i + 1)
                wait(act, hh_ready[k], i)
                nc.scalar.activation(sg[k][:, :], gu_ps[k % 2][:, 0:I], ACT.Silu).then_inc(sg_ready[k], 1)
                wait(act, xg_in[k], 16 * (i + 1))
                nc.scalar.activation(th[k][:, :], rows_of(t)[:, GAP:GAP + 1], ACT.Tanh, scale=0.5).then_inc(th_ready[k], 1)

            def step3(t, s):
                if live(s, 2):
                    evacuate3(ahead(t, 2))
                if live(s, 1):
                    silu(ahead(t, 1))

            evacuate3((0, 0))
            evacuate3((0, 1))
            silu((0, 0))
            run_tiles(act, step3)

        @blk.tensor
        def _(pe):
            pe.wait_ge(const_in, 16)

            def router_to_channels():
                pe.wait_ge(rwt_tr, 1)
                for g in range(G):
                    last = nc.tensor.transpose(rwt_ps[:, g, :], rwc[:, g * P:(g + 1) * P], kc[0:E, K_ID:K_ID + E])
                last.then_inc(rwt_tr, 1)

            def rows(t):
                i, h = t
                pi, ph = back(t, 1, 2)
                wait(pe, x2t_ready[h], 2 * i + 2)
                wait(pe, logit_read[ph], pi + 1)
                for j in range(JT):
                    for g in range(G):
                        last = nc.tensor.matmul(logit_ps[:, j, :], x2t[h][:, g, j * P:(j + 1) * P], rwt[:, g, :],
                                                start=(g == 0), stop=(g == G - 1))
                last.then_inc(logit_ready[h], 1)
                for q in range(2):
                    wait(pe, rows_read[ph], 2 * pi + q + 1)
                    for j in range(2):
                        cols = slice((2 * q + j) * P, (2 * q + j + 1) * P)
                        for g in range(G):
                            last = nc.tensor.transpose(rows_ps[q][:, j, g * P:(g + 1) * P], x2t[h][:, g, cols], ident)
                    last.then_inc(rows_ready[h], 1)

            def read_out(t):
                i, h = t
                pi, ph = back(t, 1, 2)
                for g in range(G):
                    wait(pe, sv_ready[h], 2 * i + g + 1)
                    wait(pe, y_ready[ph], 2 * pi + g + 1)
                    nc.tensor.matmul(num_ps[g][:, :], diag[:, g, :], ev[h][:, g, :], start=True, stop=False)
                    nc.tensor.matmul(by_seq(num_ps[g][:, :])[:, :, 1:T], ident,
                                     by_seq(sv[h][:, g, :])[:, :, 0:T - 1],
                                     start=False, stop=True).then_inc(num_ready[h], 1)

            def to_channels(t):
                i, h = t
                pi, ph = back(t, 1, 2)
                wait(pe, xn_ready[h], 2 * i + 2)
                for g in range(G):
                    wait(pe, eb_ready[ph], 2 * pi + g + 1)
                    for j in range(JT):
                        last = nc.tensor.transpose(kt_ps[g][:, j * P:(j + 1) * P], xn[h][:, j, g * P:(g + 1) * P], ident)
                    last.then_inc(kt_ready[h], 1)

            def step(t, s):
                if active(s, 2):
                    read_out(back(t, 2, 2))
                if active(s, 3):
                    rows(back(t, 3, 2))
                if active(s, 0):
                    to_channels(t)

            run_blocks(step, 0, 2)
            router_to_channels()
            pe.wait_ge(diag_ready, 1)
            run_blocks(step, 2, 3)
            pe.wait_ge(rwt_ready, 1)
            run_blocks(step, 3, STEPS)

            pe.wait_ge(hot_ready, 2)
            nc.tensor.matmul(bank[0][:, 0:E * NT], order_b[:, :], hot[:, :, :].rearrange("p e i -> p (e i)"), start=True, stop=True)
            nc.tensor.matmul(tot_ps, one_b[:, :], hot[:, :, :].rearrange("p e i -> p (e i)"),
                             start=True, stop=True).then_inc(rank_ready, 1)
            pe.wait_ge(num_hi_ready, 2)
            chunks = [(LO_DVE[0], at_lo_dve, 1), (LO_ACT[0], at_lo_act, 1), (LO_DVE[1], at_lo_dve, 2),
                      (LO_DVE[2], at_lo_dve, 3), (LO_ACT[1], at_lo_act, 2)]
            for c, ((a, b), ready, count) in enumerate(chunks):
                pe.wait_ge(ready, count)
                for n in range(a, b):
                    last = nc.tensor.matmul(id_ps, at_lo[:, n, :], num_hi[:, n, :, :].rearrange("p a t -> p (a t)"),
                                            start=(c == 0 and n == a), stop=(c == len(chunks) - 1 and n == b - 1))
            last.then_inc(id_ready, 1)

            pe.wait_ge(word_ready, 1)
            pe.wait_ge(wgu_in, 16 * E)
            pe.wait_ge(wdn_in, 16 * E)

            wgu_flat = wgu[:, :, :, :].rearrange("p g e n -> p g (e n)")
            wdn_flat = wdn[:, :, :, :].rearrange("p a e n -> p a (e n)")

            def transpose_x(t):
                i, k = t
                bi, bk = back(t, 2, 4)
                wait(pe, ng_ready[k], i + 1)
                wait(pe, ngt_ready[bk], bi + 1)
                for g in range(G):
                    last = nc.tensor.transpose(ngt_ps[k % 2][:, g * P:(g + 1) * P], ng[k][:, g * P:(g + 1) * P], ident)
                last.then_inc(ngt_tr[k], 1)

            def round_experts(i):
                packed = nc.values_load(word[0:1, bass.ds(i, 1)], engines=[mybir.EngineType.PE], min_val=0,
                                        max_val=(1 << 5 * BITS) - 1,
                                        skip_runtime_bounds_check_because="five sums of E - 1 comparisons")
                return [(packed >> BITS * k) & (E - 1) for k in range(5)]

            def offsets(t, s):
                k = t[1]
                if live(s, 1):
                    gate_at[0] = pe.snap(expert[k + 1] * (2 * I))
                down_at[0] = pe.snap(expert[k] * C)

            def gate_up(t, at):
                i, k = t
                bi, bk = back(t, 2, 4)
                wait(pe, ngt_ready[k], i + 1)
                wait(pe, hh_ready[bk], bi + 1)
                for g in range(G):
                    last = nc.tensor.matmul(gu_ps[k % 2][:, 0:2 * I], ngt[k][:, g, :],
                                            wgu_flat[:, g, bass.ds(at, 2 * I)],
                                            start=(g == 0), stop=(g == G - 1))
                last.then_inc(gu_ready[k], 1)

            def transpose_h(t):
                i, k = t
                bi, bk = back(t, 2, 4)
                wait(pe, hh_ready[k], i + 1)
                wait(pe, hht_ready[bk], bi + 1)
                for a in range(2):
                    last = nc.tensor.transpose(hht_ps[k % 2][0:IH, a * P:(a + 1) * P], hh[k][:, a * IH:(a + 1) * IH], ident)
                last.then_inc(hht_tr[k], 1)

            def down(t, at):
                i, k = t
                bi, bk = back(t, 2, 4)
                wait(pe, hht_ready[k], i + 1)
                wait(pe, ob_ready[bk], bi + 1)
                for a in range(2):
                    last = nc.tensor.matmul(o_ps[k % 2][:, 0:C], hht[k][:, a, :],
                                            wdn_flat[:, a, bass.ds(at, C)],
                                            start=(a == 0), stop=(a == 1))
                last.then_inc(o_ready[k], 1)

            expert = []
            gate_at, down_at = [0], [0]

            def step3(t, s):
                if t[1] == 0:
                    expert[:] = round_experts(t[0])
                offsets(t, s)
                if live(s, 2):
                    transpose_x(ahead(t, 2))
                transpose_h(t)
                if live(s, 1):
                    gate_up(ahead(t, 1), gate_at[0])
                down(t, down_at[0])

            transpose_x((0, 0))
            transpose_x((0, 1))
            gate_up((0, 0), round_experts(0)[0] * (2 * I))
            run_tiles(pe, step3)

        @blk.vector
        def _(dve):
            vec = nc.vector

            def setup_bonus():
                dve.wait_ge(wu_in, 32)
                vec.tensor_scalar_min(bonus[:, :], wu[:, 1, :], U_MAX).then_inc(setup_v, 1)
                dve.wait_ge(setup_v, 1)
                vec.tensor_scalar(down_by[:, :], bonus[:, :], -1.0, 0.0, ALU.mult, ALU.min).then_inc(setup_v, 1)

            def setup_decay():
                dve.wait_ge(fills_ready, 1)
                dve.wait_ge(exp_wu_ready, 1)
                for g in range(G):
                    last = vec.tensor_copy(by_seq(decay[g][:, :])[:, :, 1:T],
                                           exp_w[:, g:g + 1].unsqueeze(2).to_broadcast([P, SEQ, T - 1]))
                last.then_inc(decay_ready, 1)

            def setup_router():
                dve.wait_ge(rw_in, 16)
                vec.reduce_sum(rsum[:, :], rw[:, :], AX.X).then_inc(setup_v, 1)
                for g in range(G):
                    last = vec.tensor_scalar_mul(diag[:, g, :], ident, exp_u[:, g:g + 1])
                last.then_inc(diag_ready, 1)
                dve.wait_ge(setup_v, 3)
                vec.tensor_scalar_mul(rmean[:, :], rsum[:, :], 1.0 / C).then_inc(setup_v, 1)
                vec.tensor_copy(order_b[:, :], kc[:, K_ORDER:K_ORDER + P])
                vec.tensor_copy(iota_b[:, :], kc[:, K_IOTA:K_IOTA + P])
                vec.tensor_copy(tile_b[:, :], kc[:, K_TILE:K_TILE + NT])
                dve.wait_ge(setup_v, 4)
                vec.tensor_scalar_sub(rwc[:, :], rw[:, :], rmean[:, 0:1]).then_inc(rwt_tr, 1)

            def keep_router():
                dve.wait_ge(rwt_tr, 2)
                vec.tensor_copy(rwt[:, :, :], rwt_ps).then_inc(rwt_ready, 1)

            def stats1(t):
                i, h = t
                wait(dve, x_in[h], 16 * (i + 1))
                wait(dve, xn_ready[h], 2 * i)
                for j in range(JT):
                    last = vec.bn_stats(six1[h][:, j, :], xr[h][:, j, :])
                last.then_inc(six1_ready[h], 1)
                wait_apart(dve, six1_ready[h], i + 1)
                for j in range(JT):
                    last = vec.bn_aggr(mv1[h][:, j, :], six1[h][:, j, :])
                last.then_inc(mv1_ready[h], 1)

            def shift1(t):
                i, h = t
                wait(dve, rstd1_ready[h], i + 1)
                vec.scalar_tensor_tensor(out=nmr1[h][:, :], in0=mv1[h][:, :, 0], scalar=-1.0, in1=rstd1[h][:, :],
                                         op0=ALU.mult, op1=ALU.mult).then_inc(nmr1_ready[h], 1)

            def scan(t, state, data, ready, done):
                i, h = t
                wait(dve, num_ready[h] if state is sv else den_ready[h], 2 * i)
                for g in range(G):
                    wait(dve, ready[h], 2 * i + g + 1)
                    vec.tensor_tensor_scan(state[h][:, g, :], decay[g][:, :], data[h][:, g, :], 0.0,
                                           ALU.mult, ALU.add).then_inc(done[h], 1)

            def divide(t):
                i, h = t
                wait(dve, x2t_ready[h], 2 * i)
                for g in range(G):
                    wait(dve, num_ready[h], 2 * i + g + 1)
                    wait(dve, rd_ready[h], 2 * i + g + 1)
                    vec.tensor_tensor(by_seq(yt[h][:, g, :])[:, :, 1:T], by_seq(num_ps[g][:, :])[:, :, 1:T],
                                      by_seq(eb[h][:, g, :])[:, :, 1:T], ALU.mult).then_inc(y_ready[h], 1)

            def add_last(t):
                i, h = t
                wait(dve, xt_in[h], 16 * (i + 1))
                wait(dve, y0_ready[h], i + 1)
                wait(dve, rows_ready[h], 2 * i)
                wait(dve, logit_ready[h], i)
                wait(dve, y_ready[h], 2 * i + G)
                vec.tensor_tensor(x2t[h][:, 1, :], yt[h][:, 1, :], xt[h][:, 1, :], ALU.add).then_inc(x2t_ready[h], 1)

            def keep_logits(t):
                i, h = t
                wait(dve, rows_out[h], 16 * i)
                wait(dve, logit_ready[h], i + 1)
                vec.tensor_copy(logit[:, bass.ds((2 * i + h) * JT, JT), :], logit_ps)
                for j in range(JT):
                    last = vec.max(top[h][:, j, :], logit_ps[:, j, :])
                last.then_inc(logit_read[h], 1)

            def stats2(t):
                i, h = t
                for j in range(JT):
                    if j % 2 == 0:
                        wait(dve, rows_read[h], 2 * i + j // 2 + 1)
                    last = vec.bn_stats(six2[h][:, j, :], row[h][:, j, 0:C])
                last.then_inc(six2_ready[h], 1)
                wait(dve, logit_read[h], i + 1)
                vec.tensor_sub(gap[h][:, :], top[h][:, :, 0], top[h][:, :, 1]).then_inc(gap_ready[h], 1)
                wait_apart(dve, six2_ready[h], i + 1)
                for j in range(JT):
                    last = vec.bn_aggr(row[h][:, j, MEAN:RSTD + 1], six2[h][:, j, :])
                last.then_inc(mv2_ready[h], 1)

            def scale_gap(t):
                i, h = t
                wait(dve, rstd2_ready[h], i + 1)
                wait(dve, gap_ready[h], i + 1)
                vec.tensor_tensor(row[h][:, :, GAP], gap[h][:, :], row[h][:, :, RSTD], ALU.mult)\
                    .then_inc(row_ready[h], 1)

            done = [0]

            def link(ins):
                done[0] += 1
                ins.then_inc(route_v, 1)
                dve.wait_ge(route_v, done[0])

            def first_best(a, b):
                wide = [P, b - a, E]
                e8 = kc[:, K_E8:K_E8 + E].unsqueeze(1).to_broadcast(wide)
                link(vec.tensor_reduce(best[:, a:b], logit[:, a:b, :], AX.X, ALU.max))
                link(vec.tensor_tensor(is_best[:, a:b, :], logit[:, a:b, :], best[:, a:b].unsqueeze(2).to_broadcast(wide),
                                       ALU.is_ge))
                link(vec.tensor_tensor(cand[:, a:b, :], is_best[:, a:b, :], e8, ALU.mult))
                link(vec.tensor_reduce(first[:, a:b], cand[:, a:b, :], AX.X, ALU.min))
                vec.tensor_tensor(hot[:, :, a:b].rearrange("p e i -> p i e"), e8,
                                  first[:, a:b].unsqueeze(2).to_broadcast(wide), ALU.is_equal).then_inc(hot_ready, 1)

            def step(t, s):
                if active(s, 0):
                    stats1(t)
                if active(s, 5):
                    scale_gap(back(t, 5, 2))
                if active(s, 4):
                    keep_logits(back(t, 4, 2))
                    stats2(back(t, 4, 2))
                if active(s, 0):
                    shift1(t)
                if s == BLOCKS + 1:
                    for h in range(2):
                        dve.wait_ge(logit_read[h], BLOCKS // 2 - 1)
                    first_best(0, NT - 2 * JT)
                if active(s, 1):
                    scan(back(t, 1, 2), sk, ek, ek_ready, sk_ready)
                if active(s, 2):
                    divide(back(t, 2, 2))
                if active(s, 1):
                    scan(back(t, 1, 2), sv, ev, ev_ready, sv_ready)

            stats1((0, 0))
            shift1((0, 0))
            setup_bonus()
            setup_decay()
            dve.wait_ge(decay_ready, 1)
            run_blocks(step, 1, 2)
            setup_router()
            run_blocks(step, 2, 3)
            keep_router()
            run_blocks(step, 3, BLOCKS + 2)
            final = ((BLOCKS - 1) // 2, (BLOCKS - 1) % 2)
            late = back(final, 1, 2)
            add_last(final)
            scale_gap(back(final, 2, 2))
            keep_logits(late)
            stats2(late)
            keep_logits(final)
            dve.wait_ge(logit_read[0], BLOCKS // 2)
            dve.wait_ge(logit_read[1], BLOCKS // 2)
            first_best(NT - 2 * JT, NT)
            stats2(final)
            dve.wait_ge(rank_ready, 1)
            dve.wait_ge(hot_ready, 2)
            link(vec.tensor_tensor_scan(upto[:, :, :].rearrange("p e i -> p (e i)"), same_e[:, :, :].rearrange("p e i -> p (e i)"),
                                        tot_ps, 0.0, ALU.mult, ALU.add))
            link(vec.tensor_scalar(part_nt[:, :], upto[:, :, NT - 1], HALF, 1.0 / P, ALU.add, ALU.mult))
            link(vec.tensor_scalar(nt_f[:, :], part_nt[:, :], ROUNDER, ROUNDER, ALU.add, ALU.subtract))
            link(vec.tensor_tensor_scan(end_f[:, :], ones8[:, :], nt_f[:, :], 0.0, ALU.mult, ALU.add))
            link(vec.tensor_sub(base[:, :], end_f[:, :], nt_f[:, :]))
            scale_gap(late)
            scale_gap(final)
            link(vec.tensor_tensor(slot3[:, :, :], upto[:, :, :], rank_ps, ALU.add))
            link(vec.scalar_tensor_tensor(out=based[:, :, :], in0=base[:, :].unsqueeze(2).to_broadcast([P, E, NT]),
                                          scalar=float(P), in1=slot3[:, :, :], op0=ALU.mult, op1=ALU.add))
            link(vec.tensor_tensor(slot3[:, :, :], based[:, :, :], hot[:, :, :], ALU.mult))
            link(vec.reduce_sum(slot[:, :], slot3[:, :, :].rearrange("p e i -> p i e"), AX.X))
            link(vec.tensor_scalar(part_hi[:, :], slot[:, :], -HALF, 1.0 / P, ALU.add, ALU.mult))
            link(vec.tensor_scalar(hi_b[:, :], part_hi[:, :], ROUNDER, ROUNDER, ALU.add, ALU.subtract))
            vec.scalar_tensor_tensor(out=lo_b[:, :], in0=hi_b[:, :], scalar=-float(P), in1=slot[:, :],
                                     op0=ALU.mult, op1=ALU.add).then_inc(lo_ready, 1)
            per_tile = [P, NT, TILES]
            vec.tensor_tensor(at_hi[:, :, :], iota_b[:, 0:TILES].unsqueeze(1).to_broadcast(per_tile),
                              hi_b[:, :].unsqueeze(2).to_broadcast(per_tile), ALU.is_equal).then_inc(at_hi_ready, 1)
            dve.wait_ge(at_hi_ready, 1)
            vec.tensor_tensor(num_hi[:, :, 0, :], at_hi[:, :, :],
                              tile_b[:, :].unsqueeze(2).to_broadcast(per_tile), ALU.mult).then_inc(num_hi_ready, 1)
            dve.wait_ge(lo_ready, 1)
            for a, b in LO_DVE:
                vec.tensor_tensor(*lo_args(a, b), ALU.is_equal).then_inc(at_lo_dve, 1)
            dve.wait_ge(id_ready, 1)
            link(vec.tensor_scalar(id_hi[:, :], id_ps[:, 0:TILES], float(P), float(PAD_ID), ALU.mult, ALU.add))
            link(vec.tensor_tensor(id_f[:, :], id_hi[:, :], id_ps[:, TILES:2 * TILES], ALU.add))
            link(vec.tensor_copy(put_id[:, :], id_f[:, :]))
            vec.tensor_single_scalar(get_id[:, :], put_id[:, :], TOK - 1, ALU.bitwise_and).then_inc(table_ready, 1)
            shape = [1, TILES, E]
            link(vec.tensor_tensor(past[:, :, :], kc[0:1, K_IOTA:K_IOTA + TILES].unsqueeze(2).to_broadcast(shape),
                                   end_f[0:1, :].unsqueeze(1).to_broadcast(shape), ALU.is_ge))
            link(vec.reduce_sum(expert_f[:, 0:TILES], past[:, :, 0:E - 1], AX.X))
            link(vec.tensor_tensor(shifted[:, :, :], expert_f[:, 0:4 * ROUNDS].rearrange("p (r k) -> p r k", k=4),
                                   kc[0:1, K_POW:K_POW + 4].unsqueeze(1).to_broadcast([1, ROUNDS, 4]), ALU.mult))
            link(vec.reduce_sum(word_f[:, :], shifted[:, :, :], AX.X))
            vec.scalar_tensor_tensor(out=word[:, :], in0=expert_f[:, 4:4 * ROUNDS + 4:4], scalar=float(1 << 4 * BITS),
                                     in1=word_f[:, :], op0=ALU.mult, op1=ALU.add).then_inc(word_ready, 1)

            def normalise3(t):
                i, k = t
                wait(dve, xg_in[k], 16 * (i + 1))
                wait(dve, ngt_tr[k], i)
                xt_ = rows_of(t)
                vec.tensor_scalar(ng[k][:, :], xt_[:, 0:C], xt_[:, MEAN:MEAN + 1], xt_[:, RSTD:RSTD + 1],
                                  ALU.subtract, ALU.mult).then_inc(ng_ready[k], 1)

            def hidden(t):
                i, k = t
                wait(dve, sg_ready[k], i + 1)
                wait(dve, hht_tr[k], i)
                vec.tensor_tensor(hh[k][:, :], gu_ps[k % 2][:, I:2 * I], sg[k][:, :], ALU.mult).then_inc(hh_ready[k], 1)
                wait(dve, th_ready[k], i + 1)
                vec.tensor_scalar(wt[k][:, :], th[k][:, :], 0.5, 0.5, ALU.mult, ALU.add).then_inc(wt_ready[k], 1)

            def evacuate_h(t):
                i, k = t
                wait(dve, hht_tr[k], i + 1)
                wait(dve, o_ready[k], i)
                vec.tensor_copy(hht[k][:, :, :], hht_ps[k % 2][0:IH, 0:2 * P].rearrange("p (a n) -> p a n", a=2))\
                    .then_inc(hht_ready[k], 1)

            def finish(t):
                i, k = t
                wait(dve, o_ready[k], i + 1)
                wait(dve, wt_ready[k], i + 1)
                wait(dve, put_out[k], 16 * i)
                vec.scalar_tensor_tensor(out=ob[k][:, :], in0=o_ps[k % 2][:, 0:C], scalar=wt[k][:, 0:1],
                                         in1=rows_of(t)[:, 0:C], op0=ALU.mult, op1=ALU.add).then_inc(ob_ready[k], 1)

            def step3(t, s):
                if live(s, 3):
                    normalise3(ahead(t, 3))
                evacuate_h(t)
                if live(s, 1):
                    hidden(ahead(t, 1))
                finish(t)

            for s in range(3):
                normalise3((0, s))
            hidden((0, 0))
            run_tiles(dve, step3)


def kernel(x, ctx_2048, L0_xattn_w, L0_xattn_u, L0_ffn_router_w, L0_ffn_gate_w, L0_ffn_up_w, L0_ffn_down_w):
    import concourse.bacc as bacc
    from concourse.bass_utils import run_bass_kernel_spmd

    def dense(a):
        return np.ascontiguousarray(a)

    x, c = np.asarray(x).reshape(TOK, C), np.asarray(ctx_2048).reshape(TOK, C)
    gate_up = np.concatenate([np.asarray(L0_ffn_gate_w), np.asarray(L0_ffn_up_w)], axis=1)
    arrays = {
        "x": dense(x),
        "x_t": dense(x.T),
        "ctx_t": dense(c.T),
        "w": dense(np.asarray(L0_xattn_w).reshape(G, P).T),
        "u": dense(np.asarray(L0_xattn_u).reshape(G, P).T),
        "router": dense(L0_ffn_router_w),
        "gate_up_t": dense(gate_up.transpose(2, 0, 1)),
        "down_t": dense(np.asarray(L0_ffn_down_w).transpose(2, 0, 1)),
        "consts": constants(),
    }
    nc = bacc.Bacc("TRN2", target_bir_lowering=False, num_devices=1)
    args = [nc.dram_tensor(n, a.shape, mybir.dt.from_np(a.dtype), kind="ExternalInput").ap() for n, a in arrays.items()]
    out = nc.dram_tensor("out", (TOK, C), F32, kind="ExternalOutput").ap()
    build(nc, *args, out)
    r = run_bass_kernel_spmd(nc, [arrays], core_ids=[0])
    return r.results[0]["out"].reshape(B, T, C)
```
